# Optimizing a Trainium2 kernel written in Bass

```python
import numpy as np
import jax
import jax.numpy as jnp

def _softmax(x, axis=-1):
    return jax.nn.softmax(x, axis=axis)

def _gelu(x):
    return jax.nn.gelu(x, approximate=True)

def _silu(x):
    return jax.nn.silu(x)

def _sigmoid(x):
    return jax.nn.sigmoid(x)

def _layernorm(x, axis=-1, eps=1e-05):
    m = jnp.mean(x, axis=axis, keepdims=True)
    v = jnp.var(x, axis=axis, keepdims=True)
    return (x - m) / jnp.sqrt(v + eps)

def _scatter_add(tgt, idx, src, axis=0):
    return tgt.at[idx].add(src)

def _segment_sum(src, seg, n):
    return jax.ops.segment_sum(src, seg, n)
kernel_name = 'mk_adaln_d1_jaxref_r4_9b581e'

def setup_inputs(seed: int=0):
    np.random.seed(seed)
    _w = jnp.asarray

    def _L0_attn_setup():
        import math
        import jax, jax.numpy as jnp
        import numpy as np
        N_HEADS = 16

        def _alibi_slopes(n_heads: int) -> np.ndarray:

            def pow2_slopes(n):
                start = 2 ** (-2 ** (-(math.log2(n) - 3)))
                return [start * start ** i for i in range(n)]
            if math.log2(n_heads).is_integer():
                slopes = pow2_slopes(n_heads)
            else:
                closest = 2 ** math.floor(math.log2(n_heads))
                slopes = pow2_slopes(closest)
                extra = pow2_slopes(2 * closest)[0::2]
                slopes = slopes + extra[:n_heads - closest]
            return np.asarray(slopes, dtype=np.float32)

        def _build_alibi_bias(n_heads: int, T: int) -> jnp.ndarray:
            slopes = jnp.asarray(_alibi_slopes(n_heads))
            pos = jnp.arange(T)
            dist = pos[None, :] - pos[None, :].T
            causal = dist < 0
            dist = pos[None, :] - pos[:, None]
            causal = dist > 0
            d = pos[None, :] - pos[:, None]
            mask = d < 0
            bias = -slopes[:, None, None] * jnp.abs(d).astype(jnp.float32)[None, :, :]
            bias = jnp.where(mask[None, :, :], -jnp.inf, bias)
            return bias[None]
        key = jax.random.key(seed)
        k1, k2, k3 = jax.random.split(key, 3)
        B, T, D = (2, 512, 256)
        x = jax.random.normal(k1, (B, T, D), dtype=jnp.float32)
        W_qkv = jax.random.normal(k2, (D, 3 * D), dtype=jnp.float32) * (1.0 / math.sqrt(D))
        W_out = jax.random.normal(k3, (D, D), dtype=jnp.float32) * (1.0 / math.sqrt(D))
        return {'x': x, 'W_qkv': W_qkv, 'W_out': W_out}
    _L0_attn_in = _L0_attn_setup()

    def _L0_ffn_setup():
        import jax, jax.numpy as jnp
        import numpy as np
        DIM = 256
        DEPTH = 2
        HEADS = 8
        DIM_HEAD = 64
        WINDOW = 128
        INNER = HEADS * DIM_HEAD
        HID = int(DIM * 4 * 2 / 3)
        B, N = (2, 2048)
        QK_SCALE = 8.0

        def shift_token(t):
            t1, t2 = jnp.split(t, 2, axis=-1)
            t2 = jnp.pad(t2, ((0, 0), (1, 0), (0, 0)))[:, :-1]
            return jnp.concatenate([t1, t2], axis=-1)

        def l2norm(t):
            return t / jnp.clip(jnp.linalg.norm(t, axis=-1, keepdims=True), 1e-12)

        def rotate_half(x):
            x1, x2 = jnp.split(x, 2, axis=-1)
            return jnp.concatenate([-x2, x1], axis=-1)

        def rotary_xpos(q, k):
            n = q.shape[-2]
            half_idx = jnp.arange(0, DIM_HEAD, 2, dtype=jnp.float32)
            inv_freq = 1.0 / 10000.0 ** (half_idx / DIM_HEAD)
            t = jnp.arange(n, dtype=jnp.float32)
            freqs = t[:, None] * inv_freq[None, :]
            freqs = jnp.concatenate([freqs, freqs], axis=-1)
            base = (half_idx + 0.4 * DIM_HEAD) / (1.4 * DIM_HEAD)
            power = (t - n // 2) / float(WINDOW // 2)
            scale = base[None, :] ** power[:, None]
            scale = jnp.concatenate([scale, scale], axis=-1)
            cos, sin = (jnp.cos(freqs), jnp.sin(freqs))
            q = q * cos * scale + rotate_half(q) * sin * scale
            k = k * cos / scale + rotate_half(k) * sin / scale
            return (q, k)

        def local_attention(q, k, v):
            b, h, n, d = q.shape
            w = n // WINDOW
            bq = q.reshape(b, h, w, WINDOW, d) * QK_SCALE
            bk = k.reshape(b, h, w, WINDOW, d)
            bv = v.reshape(b, h, w, WINDOW, d)

            def look_around(t):
                p = jnp.pad(t, ((0, 0), (0, 0), (1, 0), (0, 0), (0, 0)))
                return jnp.concatenate([p[:, :, :w], p[:, :, 1:]], axis=3)
            bk, bv = (look_around(bk), look_around(bv))
            bt = jnp.arange(n).reshape(w, WINDOW)
            btp = jnp.pad(bt, ((1, 0), (0, 0)), constant_values=-1)
            btk = jnp.concatenate([btp[:w], btp[1:]], axis=1)
            sim = jnp.einsum('bhwid,bhwjd->bhwij', bq, bk)
            i = bt[:, :, None]
            j = btk[:, None, :]
            mask = (i < j) | (i > j + WINDOW) | (j == -1)
            sim = jnp.where(mask, -jnp.finfo(sim.dtype).max, sim)
            attn = jax.nn.softmax(sim, axis=-1)
            out = jnp.einsum('bhwij,bhwjd->bhwid', attn, bv)
            return out.reshape(b, h, n, d)

        def _layer(x, wqkv, qs, ksc, wo, lg, lb, w1, b1, w2, b2):
            b, n, _ = x.shape
            h = shift_token(x)
            qkv = h @ wqkv
            q, k, v = jnp.split(qkv, 3, axis=-1)
            to_heads = lambda t: t.reshape(b, n, HEADS, DIM_HEAD).transpose(0, 2, 1, 3)
            q, k, v = (to_heads(q), to_heads(k), to_heads(v))
            q = l2norm(q) * qs
            k = l2norm(k) * ksc
            q, k = rotary_xpos(q, k)
            o = local_attention(q, k, v)
            o = o.transpose(0, 2, 1, 3).reshape(b, n, INNER)
            x = x + o @ wo
            h = shift_token(x)
            mu = h.mean(-1, keepdims=True)
            var = h.var(-1, keepdims=True)
            h = (h - mu) / jnp.sqrt(var + 1e-05) * lg + lb
            h = h @ w1 + b1
            a, g = jnp.split(h, 2, axis=-1)
            h = a * jax.nn.gelu(g, approximate=False)
            x = x + h @ w2 + b2
            return x
        key = jax.random.key(seed)
        ks = jax.random.split(key, 6)
        return {'x': jax.random.normal(ks[0], (B, N, DIM), jnp.float32), 'wqkv': jax.random.normal(ks[1], (DEPTH, DIM, 3 * INNER), jnp.float32) * 0.02, 'q_scale': jnp.ones((DEPTH, DIM_HEAD), jnp.float32), 'k_scale': jnp.ones((DEPTH, DIM_HEAD), jnp.float32), 'wo': jax.random.normal(ks[2], (DEPTH, INNER, DIM), jnp.float32) * 0.02, 'ln_g': jnp.ones((DEPTH, DIM), jnp.float32), 'ln_b': jnp.zeros((DEPTH, DIM), jnp.float32), 'w1': jax.random.normal(ks[3], (DEPTH, DIM, 2 * HID), jnp.float32) * 0.02, 'b1': jnp.zeros((DEPTH, 2 * HID), jnp.float32), 'w2': jax.random.normal(ks[4], (DEPTH, HID, DIM), jnp.float32) * 0.02, 'b2': jnp.zeros((DEPTH, DIM), jnp.float32)}
    _L0_ffn_in = _L0_ffn_setup()
    _L0_c = _w((lambda *s: np.random.randn(*s).astype(np.float32) * 0.05)(8, 256))
    _L0_wmod = _w((lambda *s: np.random.randn(*s).astype(np.float32) * 0.05)(256, 6 * 256) * 256 ** (-0.5))
    _d = {'L0_attn_x': _L0_attn_in['x'], 'L0_attn_W_qkv': _L0_attn_in['W_qkv'], 'L0_attn_W_out': _L0_attn_in['W_out'], 'L0_ffn_wqkv': _L0_ffn_in['wqkv'], 'L0_ffn_q_scale': _L0_ffn_in['q_scale'], 'L0_ffn_k_scale': _L0_ffn_in['k_scale'], 'L0_ffn_wo': _L0_ffn_in['wo'], 'L0_ffn_ln_g': _L0_ffn_in['ln_g'], 'L0_ffn_ln_b': _L0_ffn_in['ln_b'], 'L0_ffn_w1': _L0_ffn_in['w1'], 'L0_ffn_b1': _L0_ffn_in['b1'], 'L0_ffn_w2': _L0_ffn_in['w2'], 'L0_ffn_b2': _L0_ffn_in['b2'], 'L0_c': _L0_c, 'L0_wmod': _L0_wmod}
    _x0 = _d['L0_attn_x']
    _d['L0_attn_x'] = jax.random.normal(jax.random.fold_in(jax.random.key(seed), 1), (8, 512, 256), dtype=_x0.dtype)
    del _x0
    return _d

def reference(L0_attn_x, L0_attn_W_qkv, L0_attn_W_out, L0_ffn_wqkv, L0_ffn_q_scale, L0_ffn_k_scale, L0_ffn_wo, L0_ffn_ln_g, L0_ffn_ln_b, L0_ffn_w1, L0_ffn_b1, L0_ffn_w2, L0_ffn_b2, L0_c, L0_wmod):

    def _L0_attn_ref(x, W_qkv, W_out):
        import math
        import jax, jax.numpy as jnp
        import numpy as np
        N_HEADS = 16

        def _alibi_slopes(n_heads: int) -> np.ndarray:

            def pow2_slopes(n):
                start = 2 ** (-2 ** (-(math.log2(n) - 3)))
                return [start * start ** i for i in range(n)]
            if math.log2(n_heads).is_integer():
                slopes = pow2_slopes(n_heads)
            else:
                closest = 2 ** math.floor(math.log2(n_heads))
                slopes = pow2_slopes(closest)
                extra = pow2_slopes(2 * closest)[0::2]
                slopes = slopes + extra[:n_heads - closest]
            return np.asarray(slopes, dtype=np.float32)

        def _build_alibi_bias(n_heads: int, T: int) -> jnp.ndarray:
            slopes = jnp.asarray(_alibi_slopes(n_heads))
            pos = jnp.arange(T)
            dist = pos[None, :] - pos[None, :].T
            causal = dist < 0
            dist = pos[None, :] - pos[:, None]
            causal = dist > 0
            d = pos[None, :] - pos[:, None]
            mask = d < 0
            bias = -slopes[:, None, None] * jnp.abs(d).astype(jnp.float32)[None, :, :]
            bias = jnp.where(mask[None, :, :], -jnp.inf, bias)
            return bias[None]
        B, T, D = x.shape
        H = N_HEADS
        hd = D // H
        qkv = x @ W_qkv
        q, k, v = jnp.split(qkv, 3, axis=-1)
        q = q.reshape(B, T, H, hd).transpose(0, 2, 1, 3)
        k = k.reshape(B, T, H, hd).transpose(0, 2, 1, 3)
        v = v.reshape(B, T, H, hd).transpose(0, 2, 1, 3)
        scale = 1.0 / math.sqrt(hd)
        attn = jnp.einsum('bhqd,bhkd->bhqk', q, k) * scale
        attn = attn + _build_alibi_bias(H, T)
        attn = jax.nn.softmax(attn, axis=-1)
        out = jnp.einsum('bhqk,bhkd->bhqd', attn, v)
        out = out.transpose(0, 2, 1, 3).reshape(B, T, D)
        return out @ W_out

    def _L0_ffn_ref(x, wqkv, q_scale, k_scale, wo, ln_g, ln_b, w1, b1, w2, b2):
        import jax, jax.numpy as jnp
        import numpy as np
        DIM = 256
        DEPTH = 2
        HEADS = 8
        DIM_HEAD = 64
        WINDOW = 128
        INNER = HEADS * DIM_HEAD
        HID = int(DIM * 4 * 2 / 3)
        B, N = (2, 2048)
        QK_SCALE = 8.0

        def shift_token(t):
            t1, t2 = jnp.split(t, 2, axis=-1)
            t2 = jnp.pad(t2, ((0, 0), (1, 0), (0, 0)))[:, :-1]
            return jnp.concatenate([t1, t2], axis=-1)

        def l2norm(t):
            return t / jnp.clip(jnp.linalg.norm(t, axis=-1, keepdims=True), 1e-12)

        def rotate_half(x):
            x1, x2 = jnp.split(x, 2, axis=-1)
            return jnp.concatenate([-x2, x1], axis=-1)

        def rotary_xpos(q, k):
            n = q.shape[-2]
            half_idx = jnp.arange(0, DIM_HEAD, 2, dtype=jnp.float32)
            inv_freq = 1.0 / 10000.0 ** (half_idx / DIM_HEAD)
            t = jnp.arange(n, dtype=jnp.float32)
            freqs = t[:, None] * inv_freq[None, :]
            freqs = jnp.concatenate([freqs, freqs], axis=-1)
            base = (half_idx + 0.4 * DIM_HEAD) / (1.4 * DIM_HEAD)
            power = (t - n // 2) / float(WINDOW // 2)
            scale = base[None, :] ** power[:, None]
            scale = jnp.concatenate([scale, scale], axis=-1)
            cos, sin = (jnp.cos(freqs), jnp.sin(freqs))
            q = q * cos * scale + rotate_half(q) * sin * scale
            k = k * cos / scale + rotate_half(k) * sin / scale
            return (q, k)

        def local_attention(q, k, v):
            b, h, n, d = q.shape
            w = n // WINDOW
            bq = q.reshape(b, h, w, WINDOW, d) * QK_SCALE
            bk = k.reshape(b, h, w, WINDOW, d)
            bv = v.reshape(b, h, w, WINDOW, d)

            def look_around(t):
                p = jnp.pad(t, ((0, 0), (0, 0), (1, 0), (0, 0), (0, 0)))
                return jnp.concatenate([p[:, :, :w], p[:, :, 1:]], axis=3)
            bk, bv = (look_around(bk), look_around(bv))
            bt = jnp.arange(n).reshape(w, WINDOW)
            btp = jnp.pad(bt, ((1, 0), (0, 0)), constant_values=-1)
            btk = jnp.concatenate([btp[:w], btp[1:]], axis=1)
            sim = jnp.einsum('bhwid,bhwjd->bhwij', bq, bk)
            i = bt[:, :, None]
            j = btk[:, None, :]
            mask = (i < j) | (i > j + WINDOW) | (j == -1)
            sim = jnp.where(mask, -jnp.finfo(sim.dtype).max, sim)
            attn = jax.nn.softmax(sim, axis=-1)
            out = jnp.einsum('bhwij,bhwjd->bhwid', attn, bv)
            return out.reshape(b, h, n, d)

        def _layer(x, wqkv, qs, ksc, wo, lg, lb, w1, b1, w2, b2):
            b, n, _ = x.shape
            h = shift_token(x)
            qkv = h @ wqkv
            q, k, v = jnp.split(qkv, 3, axis=-1)
            to_heads = lambda t: t.reshape(b, n, HEADS, DIM_HEAD).transpose(0, 2, 1, 3)
            q, k, v = (to_heads(q), to_heads(k), to_heads(v))
            q = l2norm(q) * qs
            k = l2norm(k) * ksc
            q, k = rotary_xpos(q, k)
            o = local_attention(q, k, v)
            o = o.transpose(0, 2, 1, 3).reshape(b, n, INNER)
            x = x + o @ wo
            h = shift_token(x)
            mu = h.mean(-1, keepdims=True)
            var = h.var(-1, keepdims=True)
            h = (h - mu) / jnp.sqrt(var + 1e-05) * lg + lb
            h = h @ w1 + b1
            a, g = jnp.split(h, 2, axis=-1)
            h = a * jax.nn.gelu(g, approximate=False)
            x = x + h @ w2 + b2
            return x
        for l in range(DEPTH):
            x = _layer(x, wqkv[l], q_scale[l], k_scale[l], wo[l], ln_g[l], ln_b[l], w1[l], b1[l], w2[l], b2[l])
        return x
    x = L0_attn_x
    mod = (_silu(L0_c) @ L0_wmod).reshape(L0_c.shape[0], 6, 1, -1)
    sa, ca, ga, sb, cb, gb = (mod[:, 0], mod[:, 1], mod[:, 2], mod[:, 3], mod[:, 4], mod[:, 5])
    ga = (2 * (ga >= 0) - 1) * jnp.maximum(jnp.abs(ga), 0.25)
    gb = (2 * (gb >= 0) - 1) * jnp.maximum(jnp.abs(gb), 0.25)
    h = _layernorm(x, axis=-1) * (1 + ca) + sa
    x = x + ga * _L0_attn_ref(h, L0_attn_W_qkv, L0_attn_W_out)
    h = _layernorm(x, axis=-1) * (1 + cb) + sb
    x = x + gb * _L0_ffn_ref(h, L0_ffn_wqkv, L0_ffn_q_scale, L0_ffn_k_scale, L0_ffn_wo, L0_ffn_ln_g, L0_ffn_ln_b, L0_ffn_w1, L0_ffn_b1, L0_ffn_w2, L0_ffn_b2)
    return x

_drawn_inputs = setup_inputs


def setup_inputs(seed=0):
    import zlib

    import numpy as np

    out = dict(_drawn_inputs(seed))
    spreads = {'L0_ffn_q_scale': (1.0, 0.6),
     'L0_ffn_k_scale': (1.0, 0.6),
     'L0_ffn_ln_g': (1.0, 0.6),
     'L0_ffn_ln_b': (0.0, 0.8),
     'L0_ffn_b1': (0.0, 0.8),
     'L0_ffn_b2': (0.0, 0.458)}
    factors = {'L0_ffn_wqkv': 6.27, 'L0_ffn_wo': 6.179, 'L0_ffn_w1': 4.783, 'L0_ffn_w2': 4.767}
    for name, (base, spread) in spreads.items():
        noise = np.random.default_rng([zlib.crc32(name.encode()), seed]).standard_normal(out[name].shape)
        drawn = base * np.exp(spread * noise) if base else spread * noise
        out[name] = jnp.asarray(drawn.astype(out[name].dtype))
    for name, factor in factors.items():
        out[name] = (out[name] * factor).astype(out[name].dtype)
    return out
```

```python
from contextlib import ExitStack

import concourse.bass as bass
from concourse import mybir

ALU = mybir.AluOpType
ACT = mybir.ActivationFunctionType
AX_X = mybir.AxisListType.X
F32 = mybir.dt.float32
F32R = mybir.dt.float32r
BF16 = mybir.dt.bfloat16

P = 128
NEG = -1e30
EPS = 1e-5


def slopes(heads):
    start = 2.0 ** (-8.0 / heads)
    return [start ** (h + 1) for h in range(heads)]


def adaln_block(nc, x_in, wqkv1_in, wout_in, wqkv2_in, qs_in, ks_in, wo_in, lng_in, lnb_in,
                w1_in, b1_in, w2_in, b2_in, c_in, wmod_in, square_in, aug_in, select_in, rot_in, kscale_in, out):
    B, T, D = x_in.shape
    NT = T // P
    KD = D // P
    H1 = 16
    HD1 = D // H1
    DEPTH, _, W3 = wqkv2_in.shape
    INNER = W3 // 3
    HD2 = qs_in.shape[1]
    H2 = INNER // HD2
    HID = w2_in.shape[1]
    HT = (HID + P - 1) // P
    HREST = HID - (HT - 1) * P
    QK_SCALE = 8.0
    G = 4
    NG1 = H1 // G
    SLOPE = slopes(H1)
    STACK = 64 + aug_in.shape[0]
    RING = 3
    POS_ROW = 64

    with ExitStack() as ctx:
        def sb(name, shape, dt=F32):
            return ctx.enter_context(nc.sbuf_tensor(name, shape, dt))

        per_batch, first = {}, {}

        def sem(name, per=0, before=0):
            s = ctx.enter_context(nc.semaphore(name))
            per_batch[id(s)], first[id(s)] = per, before
            return s

        bank = [ctx.enter_context(nc.psum_tensor(f"bank{n}", [P, 512], F32)) for n in range(8)]

        square = sb("square", [P, 8, P])
        ident = square[:, 0, :]
        down, down_wrap, up, up_wrap = (square[:, n, :] for n in range(4, 8))
        ident_bf = sb("ident_bf", [P, P], BF16)
        ones_bf = sb("ones_bf", [P, P], BF16)
        low_bf = sb("low_bf", [P, P], BF16)
        upp_bf = sb("upp_bf", [P, P], BF16)
        mask_q2 = sb("mask_q2", [P, 6, P], BF16)
        mask_t2 = sb("mask_t2", [P, 4, P], BF16)
        ones32 = sb("ones32", [P, 32])
        aug = sb("aug", [P, 2, T], F32R)
        select = sb("select", [P, 4, P], F32R)
        half_power = sb("half_power", [P, 2 * H2])
        rot = sb("rot", [P, DEPTH, 4, NT, HD2])

        wqkv1 = sb("wqkv1", [P, KD, 3 * D])
        wout = sb("wout", [P, KD, D])
        wout_g = sb("wout_g", [P, KD, D])
        wqkv2 = sb("wqkv2", [P, KD, W3])
        wo = sb("wo", [P, INNER // P, D])
        w1 = sb("w1", [P, KD, 2 * HID])
        w2 = sb("w2", [P, HT, D])
        b1 = sb("b1", [P, DEPTH, 2, HT])
        b2 = sb("b2", [P, DEPTH, D])
        lng = sb("lng", [P, DEPTH, KD])
        lnb = sb("lnb", [P, DEPTH, KD])

        mod_col = sb("mod_col", [P, 2, KD])
        mod_row = sb("mod_row", [P, 4, D])
        silu_t = sb("silu_t", [P, KD, B])
        mod_dram = nc.dram_tensor("mod_scratch", [B, 6 * D], F32).ap()

        x_res = sb("x_res", [P, NT, D])
        x_ffn = sb("x_ffn", [P, NT, D])
        y = sb("y", [P, NT, D])
        hT = sb("hT", [P, KD, T])
        stats = sb("stats", [P, NT, 2, 6])
        mv = sb("mv", [P, 5, 2])
        wait_word = sb("wait_word", [P, 1])
        zero_one = sb("zero_one", [P, 2])
        mv1 = sb("mv1", [P, NT, 2])
        small = sb("small", [P, 8, NT])
        shift_up = sb("shift_up", [P, 2, 5])
        rstd = sb("rstd", [P, NT])
        neg_max = sb("neg_max", [P, 2, G, NT])
        neg_max2 = sb("neg_max2", [P, 2, NT])
        diag = sb("diag", [P, G, T], BF16)
        ssq = sb("ssq", [P, 2, 2 * H2])
        rnorm = sb("rnorm", [P, 2, 2 * H2])
        rden = sb("rden", [P, 2, NT * G])

        stack = sb("stack", [P, (8 + 8 * RING) * T], F32R)
        high1 = stack[:, 0:4 * T].rearrange("p (j t) -> p j t", j=4)
        low1 = stack[:, 4 * T:8 * T].rearrange("p (j t) -> p j t", j=4)
        q_ring, k_ring = ([stack[:, (8 + 8 * g + 4 * n) * T:(12 + 8 * g + 4 * n) * T].rearrange("p (h t) -> p h t", h=G)
                           for g in range(RING)] for n in range(2))
        q2_stack = stack[:, 0:8 * T].rearrange("p (h t) -> p h t", h=8)
        k2_high = stack[:, 8 * T:16 * T].rearrange("p (h t) -> p h t", h=8)
        k2_low = stack[:, 16 * T:24 * T].rearrange("p (h t) -> p h t", h=8)

        scratch = sb("scratch", [P, 26 * T])

        def part(a, n, pattern, **kw):
            return scratch[:, a * T:(a + n) * T].rearrange(pattern, **kw)

        v1 = part(0, 4, "p (t h c) -> p t h c", t=NT, h=H1)
        probs1 = part(4, 8, "p (s h q) -> p s h q", s=2, h=G)
        oT1 = part(12, 2, "p (s q) -> p s q", s=2)
        on1 = part(14, 2, "p (t f) -> p t f", t=NT)
        onT1 = part(16, 2, "p (k q) -> p k q", k=KD)
        more_diag = part(18, 2, "p (s q) -> p s q", s=2).bitcast(BF16).rearrange("p s (a q) -> p (s a) q", a=2)
        diag1 = [diag[:, n, :] for n in range(G)] + [more_diag[:, n, :] for n in range(G)]
        q2 = part(0, 4, "p (t f) -> p t f", t=NT)
        k2 = part(4, 4, "p (t f) -> p t f", t=NT)
        rot_c = part(8, 2, "p (s f) -> p s f", s=2)
        rot_s = part(10, 2, "p (s f) -> p s f", s=2)
        sq = part(12, 2, "p (s f) -> p s f", s=2)
        v2 = part(14, 4, "p (t f) -> p t f", t=NT)
        probs2 = [part(a, 2, "p (s q) -> p (s q)", s=1) for a in (8, 10, 12, 18)]
        oT2 = part(20, 4, "p (k q) -> p k q", k=H2 // 2)
        denT2 = part(24, 2, "p (k q) -> p k q", k=H2 // G)
        on2 = q2
        onT2 = part(4, 4, "p (k q) -> p k q", k=H2 // 2)
        gate = part(0, 2, "p (s q) -> p s q", s=2)
        u = part(2, HT, "p (m q) -> p m q", m=HT)
        wmod = scratch[:, 0:KD * 6 * D].rearrange("p (k n) -> p k n", k=KD)
        mod_rows = scratch[0:B, 12 * D:18 * D]
        mod_abs = scratch[0:B, 18 * D:19 * D]
        mod_sign = scratch[0:B, 19 * D:20 * D]
        setup_select = part(12, 1, "p (s c) -> p s c", s=4)
        setup_aug = part(13, 2, "p (s t) -> p s t", s=2)
        silu = scratch[0:B, 20 * D:23 * D].rearrange("p (a f) -> p a f", a=3)

        s_const = sem("const_loaded")
        s_cst_dve = sem("const_made")
        s_silu = sem("silu_steps")
        s_silu_e = sem("silu_exp")
        s_silu_t = sem("silu_transposed")
        s_silu_c = sem("silu_copied")
        s_mod = sem("mod_product")
        s_mod_r = sem("mod_rows_ready")
        s_mod_st = sem("mod_stored")
        VEC = 94
        s_vec = sem("vector_step", VEC)
        s_x = sem("x_loaded", 16)
        s_modc = sem("mod_columns_loaded", 32)
        s_modr = sem("mod_rows_loaded", 16)
        s_var = sem("variance_ready", 4)
        s_rstd = sem("rstd_ready", 4)
        s_y = sem("normed_ready", 3 * NT)
        s_yT = sem("normed_transposed", 1)
        s_hT = sem("features_ready", KD)
        s_qk = sem("qk_projected", 4)
        s_v = sem("v_projected", 2)
        s_high = sem("high_part_ready", 4)
        s_low = sem("low_part_ready", 4)
        s_v1 = sem("v_copied", 2)
        s_v1one = sem("v_ones_set", 1)
        s_aug = sem("position_rows_loaded", 16 * 2 * RING)
        s_sel = sem("stack_rows_ready", NG1 * G)
        s_stk = sem("stack_rows_copied", NG1 * G)
        s_s1 = sem("scores_ready", H1 * NT)
        s_m1 = sem("maximum_taken", H1 * NT)
        s_d1 = sem("diagonal_ready", H1)
        s_t1 = sem("key_scores_ready", H1 * NT)
        s_e1 = sem("probs_ready", H1 * NT)
        s_pv1 = sem("values_summed", H1)
        s_o1 = sem("heads_copied", NG1)
        s_oq1 = sem("heads_transposed", NG1)
        s_on1 = sem("heads_normed", NG1)
        s_onT1 = sem("attn_transposed", 1)
        s_onTc1 = sem("attn_features_ready", KD)
        s_wg = sem("gated_weights_ready", 1)
        s_p1 = sem("attn_out_ready", 2)
        s_x1 = sem("residual_ready", 2)
        s_xf = sem("ffn_input_ready", NT)
        s_xT = sem("stream_transposed", DEPTH)
        s_zero = sem("first_column_zeroed", DEPTH)
        s_sT = sem("shifted_ready", DEPTH * KD)
        s_qkv = sem("qkv_ready", DEPTH * 3 * NT)
        s_sq = sem("squares_ready", DEPTH * 2 * NT)
        s_rt = sem("rotated_parts_ready", DEPTH * 2 * NT)
        s_ss = sem("square_sums_ready", DEPTH * NT)
        s_rsum = sem("rotated_sum_ready", DEPTH * 2 * NT)
        s_rn = sem("inverse_norm_ready", DEPTH * NT)
        s_qn = sem("heads_scaled", DEPTH * 2 * NT)
        s_v2 = sem("v2_copied", DEPTH * NT)
        s_tq = sem("pair_transposed", DEPTH * H2)
        s_hi2 = sem("head_high_ready", DEPTH * 3 * H2)
        s_lo2 = sem("head_low_ready", DEPTH * 2 * H2)
        s_klow0 = sem("low_stacks_zeroed", 2)
        s_s2 = sem("local_scores_ready", DEPTH * 2 * H2)
        s_m2 = sem("local_maximum_taken", DEPTH * 2 * H2)
        s_d2 = sem("local_diagonal_ready", DEPTH * H2)
        s_t2 = sem("local_key_scores_ready", DEPTH * 2 * H2)
        s_e2 = sem("local_probs_ready", DEPTH * 2 * H2)
        s_pv2 = sem("local_values_summed", DEPTH * H2 // 2)
        s_o2 = sem("local_heads_copied", DEPTH * H2 // 2)
        s_dn = sem("denominators_copied", DEPTH * 2)
        s_dT = sem("denominators_transposed", DEPTH * 2)
        s_oq2 = sem("local_heads_transposed", DEPTH * NT)
        s_on2 = sem("local_heads_normed", DEPTH * NT)
        s_onT2 = sem("local_attn_transposed", DEPTH * 4)
        s_onTc2 = sem("local_attn_features_ready", DEPTH * 4)
        s_p2 = sem("local_attn_out_ready", DEPTH * 2)
        s_x2 = sem("stream_ready", DEPTH * 2)
        s_st = sem("half_stats_ready", DEPTH)
        s_dshift = sem("stats_shifted", DEPTH)
        s_up = sem("up_stats_ready", DEPTH)
        s_ushift = sem("up_stats_shifted", DEPTH)
        s_nT = sem("norm_transposed", DEPTH)
        s_nTc = sem("norm_features_ready", DEPTH * 3)
        s_g = sem("gate_product_ready", DEPTH * HT)
        s_a = sem("value_product_ready", DEPTH * HT)
        s_gl = sem("gelu_ready", DEPTH * HT)
        s_u = sem("hidden_ready", DEPTH * HT)
        s_bias = sem("stream_biased", DEPTH * 2)
        s_f = sem("ffn_out_ready", DEPTH * 2)
        s_x3 = sem("layer_done", DEPTH * 2)
        s_gx = sem("gated_stream_ready", 1, before=1)
        s_res = sem("result_ready", 1, before=1)
        s_out = sem("result_stored", 16, before=16)
        s_lw = [sem(f"layer_weights_{n}_loaded", 16 * DEPTH * (2 if n == 3 else 1)) for n in range(4)]

        def at(i, s, k):
            assert k + first[id(s)] >= 1
            return i * per_batch[id(s)] + k + first[id(s)]

        N_CONST = [0]
        block = ctx.enter_context(nc.Block())

        def load_layer(e, l, what):
            if what == 0:
                e.dma_start(wqkv2[:, :, :], wqkv2_in[l].rearrange("(k p) n -> p k n", p=P)).then_inc(s_lw[0], 16)
            if what == 1:
                e.dma_start(wo[:, :, :], wo_in[l].rearrange("(k p) n -> p k n", p=P)).then_inc(s_lw[1], 16)
            if what == 2:
                e.dma_start(w1[:, :, :], w1_in[l].rearrange("(k p) n -> p k n", p=P)).then_inc(s_lw[2], 16)
            if what == 3:
                e.dma_start(w2[:, 0:HT - 1, :], w2_in[l, 0:(HT - 1) * P, :].rearrange("(k p) n -> p k n", p=P)).then_inc(s_lw[3], 16)
                e.dma_start(w2[0:HREST, HT - 1, :], w2_in[l, (HT - 1) * P:HID, :]).then_inc(s_lw[3], 16)

        @block.sync
        def _(e):
            def c(dst, src, thin=False):
                e.dma_start(dst, src, allow_slow_non_contiguous=thin).then_inc(s_const, 16)
                N_CONST[0] += 16

            c(silu[:, 0, :], c_in)
            c(square[:, :, :], square_in)
            c(wmod, wmod_in.rearrange("(k p) n -> p k n", p=P))
            c(setup_select, select_in)
            c(setup_aug[POS_ROW:STACK, :, :], aug_in)
            c(wqkv1[:, :, :], wqkv1_in.rearrange("(k p) n -> p k n", p=P))
            c(wout[:, :, :], wout_in.rearrange("(k p) n -> p k n", p=P))
            c(x_res[:, 0, :], kscale_in.to_broadcast([P, D]))
            for l in range(DEPTH):
                c(rot[:, l, :, :, :], rot_in)
                c(b2[:, l, :], b2_in[l:l + 1, :].to_broadcast([P, D]))
                c(lng[:, l, :], lng_in[l].rearrange("(k p) -> p k", p=P), thin=True)
                c(lnb[:, l, :], lnb_in[l].rearrange("(k p) -> p k", p=P), thin=True)
                c(x_ffn[:, l, 0:HD2], qs_in[l:l + 1, :].to_broadcast([P, HD2]))
                c(x_ffn[:, l, HD2:2 * HD2], ks_in[l:l + 1, :].to_broadcast([P, HD2]))
                for half in range(2):
                    c(b1[:, l, half, 0:HT - 1],
                      b1_in[l, half * HID:half * HID + (HT - 1) * P].rearrange("(m p) -> p m", p=P), thin=True)
                    c(b1[0:HREST, l, half, HT - 1:HT],
                      b1_in[l, half * HID + (HT - 1) * P:(half + 1) * HID].rearrange("(p m) -> p m", m=1), thin=True)
            e.wait_ge(s_cst_dve, 1)
            for what in range(4):
                load_layer(e, 0, what)
            e.wait_ge(s_mod_r, 1)
            e.dma_start(mod_dram, mod_rows[:, :]).then_inc(s_mod_st, 16)
            e.wait_ge(s_mod_st, 16)

            with e.Fori(0, B) as i:
                e.wait_ge(s_res, at(i, s_res, 0))
                e.dma_start(x_res[:, :, :], x_in[bass.ds(i, 1)].rearrange("o (t p) f -> p (o t) f", p=P)).then_inc(s_x, 16)
                for n in range(2):
                    e.dma_start(mod_col[:, n, :],
                                mod_dram[bass.ds(i, 1), n * D:(n + 1) * D].rearrange("o (k p) -> p (o k)", p=P),
                                allow_slow_non_contiguous=True).then_inc(s_modc, 16)
                e.wait_ge(s_gx, at(i, s_gx, 0))
                e.dma_start(mod_row[:, :, :].rearrange("p a f -> p (a f)"),
                            mod_dram[bass.ds(i, 1), 2 * D:6 * D].to_broadcast([P, 4 * D])).then_inc(s_modr, 16)
                for g in range(RING):
                    for n, ring in enumerate((q_ring, k_ring)):
                        e.dma_start(ring[g][POS_ROW:STACK, :, :].bitcast(F32),
                                    aug[POS_ROW:STACK, n:n + 1, :].bitcast(F32).to_broadcast([STACK - POS_ROW, G, T])).then_inc(s_aug, 16)
                for l in range(DEPTH):
                    nxt = (l + 1) % DEPTH
                    e.wait_ge(s_qkv, at(i, s_qkv, 3 * NT * (l + 1)))
                    load_layer(e, nxt, 0)
                    e.wait_ge(s_p2, at(i, s_p2, 2 * (l + 1)))
                    load_layer(e, nxt, 1)
                    e.wait_ge(s_a, at(i, s_a, HT * (l + 1)))
                    load_layer(e, nxt, 2)
                    e.wait_ge(s_f, at(i, s_f, 2 * (l + 1)))
                    load_layer(e, nxt, 3)
                e.wait_ge(s_res, at(i, s_res, 1))
                e.dma_start(out[bass.ds(i, 1)].rearrange("o (t p) f -> p (o t) f", p=P), y[:, :, :]).then_inc(s_out, 16)
            e.wait_ge(s_out, 16 * B + 16)
            for n in range(4):
                e.wait_ge(s_lw[n], per_batch[id(s_lw[n])] * B + (32 if n == 3 else 16))

        @block.gpsimd
        def _(e):
            e.memset(w2[:, HT - 1, :], 0.0)
            e.memset(half_power[:, :], -0.5).then_inc(s_cst_dve, 1)
            e.memset(ones32[:, :], 1.0)
            e.memset(zero_one[:, 0:1], 0.0)
            e.memset(zero_one[:, 1:2], 1.0)
            e.memset(mv[:, 0, :], 0.0)
            e.memset(shift_up[:, 0, NT:NT + 1], 0.0)
            e.memset(ones_bf[:, :], 1.0).then_inc(s_cst_dve, 1)
            e.wait_ge(s_const, N_CONST[0])
            e.wait_ge(s_cst_dve, 2)

            with e.Fori(0, B) as i:
                def power(dst, src, width, done):
                    e.tensor_tensor(dst, src, half_power[:, 0:width], ALU.pow).then_inc(done, 1)

                def fill(dst, word):
                    n, a, b = dst.shape
                    word = word.rearrange("p (a b) -> p a b", a=1).to_broadcast([n, a, b])
                    return e.tensor_tensor(dst, word, word, ALU.mult)

                e.wait_ge(s_var, at(i, s_var, 1))
                power(rstd[:, :], small[:, 0, :], NT, s_rstd)
                e.wait_ge(s_y, at(i, s_y, 1))
                for t in range(NT):
                    ins = fill(v1[:, t, :, HD1:2 * HD1], zero_one[:, 1:2])
                ins.then_inc(s_v1one, 1)
                e.wait_ge(s_modr, at(i, s_modr, 16))
                e.tensor_tensor(wout_g[:, :, :], wout[:, :, :],
                                mod_row[:, 0:1, :].to_broadcast([P, KD, D]), ALU.mult).then_inc(s_wg, 1)
                e.wait_ge(s_x1, at(i, s_x1, 2))
                for a in range(2):
                    zero = slice(64 - 64 * a, 128 - 64 * a)
                    if a:
                        e.wait_ge(s_klow0, at(i, s_klow0, a))
                    fill(k2_low[zero, a::2, :], zero_one[zero, 0:1]).then_inc(s_klow0, 1)
                e.wait_ge(s_klow0, at(i, s_klow0, 2))
                e.wait_ge(s_var, at(i, s_var, 2))
                power(rstd[:, :], small[:, 0, :], NT, s_rstd)
                for l in range(DEPTH):
                    e.wait_ge(s_xT, at(i, s_xT, l + 1))
                    fill(hT[:, 1:2, 0:1], zero_one[:, 0:1]).then_inc(s_zero, 1)
                    for t in range(NT):
                        for n in range(2):
                            k = (l * NT + t) * 2 + n
                            dst = (q2, k2)[n]
                            e.wait_ge(s_rt, at(i, s_rt, k + 1))
                            e.tensor_tensor(dst[:, t, :], rot_c[:, n, :], rot_s[:, n, :], ALU.add).then_inc(s_rsum, 1)
                        e.wait_ge(s_ss, at(i, s_ss, l * NT + t + 1))
                        power(rnorm[:, t % 2, :], ssq[:, t % 2, :], 2 * H2, s_rn)
                    e.wait_ge(s_var, at(i, s_var, 3 + l))
                    power(rstd[:, :], small[:, 5, :], NT, s_rstd)
                    e.wait_ge(s_y, at(i, s_y, NT * (l + 2)))
                    for n in range(2):
                        e.tensor_tensor(x_ffn[:, 2 * n:2 * n + 2, :], x_ffn[:, 2 * n:2 * n + 2, :],
                                        b2[:, l:l + 1, :].to_broadcast([P, 2, D]), ALU.add).then_inc(s_bias, 1)
                e.wait_ge(s_x3, at(i, s_x3, 2 * DEPTH))
                e.wait_ge(s_out, at(i, s_out, 0))
                e.tensor_tensor(y[:, :, :], x_ffn[:, :, :],
                                mod_row[:, 3:4, :].to_broadcast([P, NT, D]), ALU.mult).then_inc(s_gx, 1)

        @block.scalar
        def _(e):
            e.wait_ge(s_const, N_CONST[0])
            e.activation(silu[:, 1, :], silu[:, 0, :], ACT.Exp, scale=-1.0).then_inc(s_silu_e, 1)

            with e.Fori(0, B) as i:
                e.wait_ge(s_yT, at(i, s_yT, 1))
                e.wait_ge(s_modc, at(i, s_modc, 32))
                for k in range(KD):
                    e.activation(hT[:, k, :], bank[k][:, :], ACT.Identity, scale=mod_col[:, 1, k:k + 1],
                                 bias=mod_col[:, 0, k:k + 1]).then_inc(s_hT, 1)
                for j in range(4):
                    e.wait_ge(s_qk, at(i, s_qk, j + 1))
                    e.activation(high1[:, j, :], bank[4 + j][:, :], ACT.Copy).then_inc(s_high, 1)
                for n in range(2):
                    e.wait_ge(s_v, at(i, s_v, n + 1))
                    e.activation(v1[:, 2 * n:2 * n + 2, :, 0:HD1],
                                 bank[2 + n][:, :].rearrange("p (t h c) -> p t h c", t=2, h=H1), ACT.Copy).then_inc(s_v1, 1)

                def stack_rows(g, which):
                    m = g * G + which
                    e.wait_ge(s_sel, at(i, s_sel, m + 1))
                    if g >= RING:
                        e.wait_ge(s_t1, at(i, s_t1, G * NT * (g - RING + 1)))
                    b = bank[m % 2 if g == 0 else 7]
                    for a in range(2):
                        ins = e.activation((q_ring, k_ring)[which % 2][g % RING][0:POS_ROW, 2 * (which // 2) + a, :],
                                           b[64 * a:64 * a + 64, :], ACT.Copy)
                    ins.then_inc(s_stk, 1)

                for which in range(2 * G):
                    stack_rows(which // G, which % G)
                n = 0
                for g in range(NG1):
                    for step, kt in enumerate(reversed(range(NT))):
                        if g * NT + step >= 2:
                            e.wait_ge(s_pv1, at(i, s_pv1, g * NT + step - 1))
                        for h in range(G):
                            n += 1
                            e.wait_ge(s_t1, at(i, s_t1, n))
                            w = (kt + 1) * P
                            e.activation(probs1[:, kt % 2, h, 0:w], bank[2 + (n - 1) % 3][:, 0:w], ACT.Exp,
                                         scale=SLOPE[g * G + h]).then_inc(s_e1, 1)
                            if h == 1 and g + 2 < NG1:
                                stack_rows(g + 2, step)
                e.wait_ge(s_onT1, at(i, s_onT1, 1))
                for k in range(KD):
                    e.activation(onT1[:, k, :], bank[k][:, :], ACT.Copy).then_inc(s_onTc1, 1)

                for l in range(DEPTH):
                    e.wait_ge(s_xT, at(i, s_xT, l + 1))
                    e.activation(hT[:, 0, :], bank[0][:, :], ACT.Copy).then_inc(s_sT, 1)
                    e.activation(hT[:, 1, 1:T], bank[1][:, 0:T - 1], ACT.Copy).then_inc(s_sT, 1)
                    for t in range(NT):
                        for n in range(2):
                            k = (l * NT + t) * 2 + n
                            e.wait_ge(s_qkv, at(i, s_qkv, (l * NT + t) * 3 + n + 1))
                            if t >= 1:
                                e.wait_ge(s_ss, at(i, s_ss, l * NT + t))
                            e.activation(sq[:, n, :], bank[2 + n + 3 * (t % 2)][:, :], ACT.Square).then_inc(s_sq, 1)
                        e.wait_ge(s_qkv, at(i, s_qkv, (l * NT + t) * 3 + 3))
                        e.activation(v2[:, t, :], bank[4 + 3 * (t % 2)][:, :], ACT.Copy).then_inc(s_v2, 1)
                    def high2(pair):
                        for n in range(2):
                            e.wait_ge(s_tq, at(i, s_tq, (l * H2 // 2 + pair) * 2 + n + 1))
                            for a in range(2):
                                src = bank[n][64 * a:64 * a + 64, :]
                                own, other = slice(64 * a, 64 * a + 64), slice(64 - 64 * a, 128 - 64 * a)
                                dst = (q2_stack, k2_high)[n]
                                e.activation(dst[own, 2 * pair + a, :], src, ACT.Copy).then_inc(s_hi2, 1)
                                if n == 1:
                                    e.activation(dst[other, 2 * pair + a, :], src, ACT.Copy).then_inc(s_hi2, 1)

                    high2(0)
                    for h in range(H2 + 1):
                        if h >= 1:
                            g = h - 1
                            if g >= 4:
                                e.wait_ge(s_pv2, at(i, s_pv2, l * H2 // 2 + (g - 4) // 2 + 1))
                            for n in range(2):
                                e.wait_ge(s_t2, at(i, s_t2, (l * H2 + g) * 2 + n + 1))
                                w = (512, 384)[n]
                                e.activation(probs2[g % 4][:, 512 * n:512 * n + w], bank[4 + n][:, 0:w],
                                             ACT.Exp).then_inc(s_e2, 1)
                        if h % 2 == 0 and h // 2 + 1 < H2 // 2:
                            high2(h // 2 + 1)
                    for k in (0, 2):
                        e.wait_ge(s_onT2, at(i, s_onT2, l * 4 + k + 1))
                        e.activation(onT2[:, k, :], bank[(6, 7, 0, 1)[k]][:, :], ACT.Copy).then_inc(s_onTc2, 1)
                    e.wait_ge(s_nT, at(i, s_nT, l + 1))
                    e.activation(hT[:, 0, :], bank[0][:, :], ACT.Identity, scale=lng[:, l, 0:1],
                                 bias=lnb[:, l, 0:1]).then_inc(s_nTc, 1)
                    e.activation(hT[:, 1, 1:T], bank[1][:, 0:T - 1], ACT.Identity, scale=lng[:, l, 1:2],
                                 bias=lnb[:, l, 1:2]).then_inc(s_nTc, 1)
                    e.activation(hT[:, 1, 0:1], bank[1][:, T - 1:T], ACT.Identity, scale=lng[:, l, 1:2],
                                 bias=lnb[:, l, 1:2]).then_inc(s_nTc, 1)
                    for m in range(HT):
                        r = P if m < HT - 1 else HREST
                        e.wait_ge(s_g, at(i, s_g, l * HT + m + 1))
                        if m >= 2:
                            e.wait_ge(s_u, at(i, s_u, l * HT + m - 1))
                        e.activation(gate[0:r, m % 2, :], bank[2 + 2 * (m % 2)][0:r, :], ACT.Gelu,
                                     bias=b1[0:r, l, 1, m:m + 1]).then_inc(s_gl, 1)

        @block.vector
        def _(e):
            e.wait_ge(s_const, N_CONST[0])
            chain = [0]

            def setup_step():
                chain[0] += 1
                return 1

            e.wait_ge(s_silu_e, 1)
            e.tensor_scalar(silu[:, 1, :], silu[:, 1, :], 1.0, None, ALU.add).then_inc(s_silu, setup_step())
            e.wait_ge(s_silu, chain[0])
            e.reciprocal(silu[:, 2, :], silu[:, 1, :]).then_inc(s_silu, setup_step())
            e.wait_ge(s_silu, chain[0])
            e.tensor_tensor(silu[:, 1, :], silu[:, 0, :], silu[:, 2, :], ALU.mult).then_inc(s_silu, setup_step())
            e.wait_ge(s_silu, chain[0])
            e.tensor_copy(select[:, :, :], setup_select)
            e.tensor_copy(aug[POS_ROW:STACK, :, :], setup_aug[POS_ROW:STACK, :, :])
            e.tensor_copy(ident_bf[:, :], ident)
            e.tensor_copy(low_bf[:, :], square[:, 1, :])
            e.tensor_copy(upp_bf[:, :], square[:, 2, :])
            for n, which in enumerate((3, 2, 1, 2, 1, 2)):
                e.tensor_copy(mask_q2[:, n, :], square[:, which, :])
            for n in range(4):
                e.tensor_copy(mask_t2[:, n, :], square[:, 1 + n % 2, :])
            e.tensor_tensor(wqkv1[:, :, D:2 * D], wqkv1[:, :, D:2 * D],
                            x_res[:, 0:1, :].to_broadcast([P, KD, D]), ALU.mult).then_inc(s_silu, setup_step())
            e.wait_ge(s_silu, chain[0])
            half = HD2 // 2
            for l in range(DEPTH):
                e.tensor_scalar(x_ffn[:, l, 0:HD2], x_ffn[:, l, 0:HD2], QK_SCALE, None, ALU.mult).then_inc(s_silu, setup_step())
                e.wait_ge(s_silu, chain[0])
                for n in range(2):
                    scale = x_ffn[:, l, n * HD2:(n + 1) * HD2]
                    e.tensor_tensor(rot[:, l, 2 * n, :, :], rot[:, l, 2 * n, :, :],
                                    scale.rearrange("p (o d) -> p o d", o=1).to_broadcast([P, NT, HD2]), ALU.mult)
                    for a in range(2):
                        dst = rot[:, l, 2 * n + 1, :, a * half:(a + 1) * half]
                        s = scale[:, (1 - a) * half:(2 - a) * half]
                        e.tensor_tensor(dst, dst, s.rearrange("p (o d) -> p o d", o=1).to_broadcast([P, NT, half]), ALU.mult)
            e.wait_ge(s_silu_t, 1)
            e.tensor_copy(silu_t[:, :, :], bank[0][:, 0:KD * B].rearrange("p (k b) -> p k b", k=KD)).then_inc(s_silu_c, 1)
            e.wait_ge(s_mod, 1)
            for n in range(3):
                e.tensor_copy(mod_rows[:, 512 * n:512 * n + 512], bank[1 + n][0:B, :]).then_inc(s_silu, setup_step())
                e.wait_ge(s_silu, chain[0])
            for n in (1, 4):
                e.tensor_scalar(mod_rows[:, n * D:(n + 1) * D], mod_rows[:, n * D:(n + 1) * D], 1.0, None, ALU.add).then_inc(s_silu, setup_step())
                e.wait_ge(s_silu, chain[0])
            for n in (2, 5):
                row = mod_rows[:, n * D:(n + 1) * D]
                e.tensor_scalar(mod_abs[:, :], row, -1.0, None, ALU.mult).then_inc(s_silu, setup_step())
                e.wait_ge(s_silu, chain[0])
                e.tensor_tensor(mod_abs[:, :], mod_abs[:, :], row, ALU.max).then_inc(s_silu, setup_step())
                e.wait_ge(s_silu, chain[0])
                e.tensor_scalar(mod_abs[:, :], mod_abs[:, :], 0.25, None, ALU.max).then_inc(s_silu, setup_step())
                e.wait_ge(s_silu, chain[0])
                e.tensor_scalar(mod_sign[:, :], row, 0.0, 2.0, ALU.is_ge, ALU.mult).then_inc(s_silu, setup_step())
                e.wait_ge(s_silu, chain[0])
                e.tensor_scalar(mod_sign[:, :], mod_sign[:, :], -1.0, None, ALU.add).then_inc(s_silu, setup_step())
                e.wait_ge(s_silu, chain[0])
                e.tensor_tensor(row, mod_abs[:, :], mod_sign[:, :], ALU.mult).then_inc(s_silu, setup_step())
                e.wait_ge(s_silu, chain[0])
            e.tensor_copy(mod_abs[:, 0:1], mod_sign[:, 0:1]).then_inc(s_mod_r, 1)
            e.memset(wait_word[:, :], 0.0).then_inc(s_gx, 1)
            e.wait_ge(s_gx, 1)
            e.memset(wait_word[:, :], 0.0).then_inc(s_res, 1)
            e.wait_ge(s_res, 1)
            e.memset(wait_word[:, :], 0.0).then_inc(s_out, 16)
            e.wait_ge(s_out, 16)

            with e.Fori(0, B) as i:
                tally = [0]

                def own_step():
                    tally[0] += 1
                    return 1

                def whole_stats(src, t0=0):
                    for t in range(NT):
                        e.bn_stats(stats[:, t, 0, :], src[:, t, :]).then_inc(s_vec, own_step())
                    e.wait_ge(s_vec, at(i, s_vec, tally[0]))
                    e.memset(wait_word[:, :], 0.0)
                    for t in range(NT):
                        e.bn_aggr(mv[:, 1 + t, :], stats[:, t, 0, :]).then_inc(s_vec, own_step())
                    e.wait_ge(s_vec, at(i, s_vec, tally[0]))
                    e.tensor_scalar(small[:, 0, :], mv[:, 1:1 + NT, 1], EPS, None, ALU.add).then_inc(s_var, 1)

                e.wait_ge(s_x, at(i, s_x, 16))
                whole_stats(x_res)
                e.wait_ge(s_out, at(i, s_out, 0))
                e.wait_ge(s_rstd, at(i, s_rstd, 1))
                for t in range(NT):
                    e.tensor_scalar(y[:, t, :], x_res[:, t, :], mv[:, 1 + t, 0:1], rstd[:, t:t + 1],
                                    ALU.subtract, ALU.mult).then_inc(s_y, 1)
                for j in range(4):
                    e.wait_ge(s_high, at(i, s_high, j + 1))
                    e.tensor_tensor(low1[:, j, :], bank[4 + j][:, :], high1[:, j, :].bitcast(F32),
                                    ALU.subtract).then_inc(s_low, 1)

                def maxima1(g, h):
                    for it in range(NT):
                        n = (g * G + h) * NT + it
                        e.wait_ge(s_s1, at(i, s_s1, n + 1))
                        e.tensor_reduce(neg_max[:, g % 2, h, it:it + 1], bank[n % 2][:, it * P:T], AX_X, ALU.max,
                                        negate=True).then_inc(s_m1, 1)
                    e.wait_ge(s_m1, at(i, s_m1, (g * G + h + 1) * NT))
                    if g >= 2:
                        e.wait_ge(s_t1, at(i, s_t1, G * NT * (g - 1)))
                    for it in range(NT):
                        ins = e.tensor_scalar(diag1[(g * G + h) % 8][:, it * P:(it + 1) * P], ident_bf[:, :],
                                              neg_max[:, g % 2, h, it:it + 1], None, ALU.mult)
                    ins.then_inc(s_d1, 1)

                def heads1(g):
                    e.wait_ge(s_oq1, at(i, s_oq1, g + 1))
                    o = bank[7][:, :].rearrange("p (t h c) -> p t h c", t=NT, h=G)
                    rd = rden[:, 0, 0:NT * G].rearrange("p (t h o) -> p t h o", t=NT, o=1)
                    e.reciprocal(rd, o[:, :, :, HD1:HD1 + 1]).then_inc(s_vec, own_step())
                    e.wait_ge(s_vec, at(i, s_vec, tally[0]))
                    e.tensor_tensor(on1[:, :, g * G * HD1:(g + 1) * G * HD1].rearrange("p t (h c) -> p t h c", h=G),
                                    o[:, :, :, 0:HD1], rd.to_broadcast([P, NT, G, HD1]), ALU.mult).then_inc(s_on1, 1)

                def copy1(g):
                    e.wait_ge(s_pv1, at(i, s_pv1, (g + 1) * NT))
                    e.tensor_copy(oT1[:, g % 2, :], bank[5 + g % 2][:, :]).then_inc(s_o1, 1)

                for h in range(G):
                    maxima1(0, h)
                for g in range(NG1):
                    for step in range(NT):
                        if step == 1 and g >= 1:
                            copy1(g - 1)
                        if step == 2 and g >= 1:
                            heads1(g - 1)
                        if g + 1 < NG1:
                            maxima1(g + 1, step)
                copy1(NG1 - 1)
                heads1(NG1 - 1)
                for n in range(2):
                    e.wait_ge(s_p1, at(i, s_p1, n + 1))
                    e.tensor_tensor(x_res[:, 2 * n:2 * n + 2, :], bank[2 + n][:, :].rearrange("p (t f) -> p t f", t=2),
                                    x_res[:, 2 * n:2 * n + 2, :], ALU.add).then_inc(s_x1, 1)
                e.wait_ge(s_x1, at(i, s_x1, 2))
                whole_stats(x_res)
                for t in range(NT):
                    e.scalar_tensor_tensor(x_ffn[:, t, :], x_res[:, t, :], mv[:, 1 + t, 0:1], mod_row[:, 2, :],
                                           ALU.subtract, ALU.mult).then_inc(s_vec, own_step())
                e.wait_ge(s_vec, at(i, s_vec, tally[0]))
                e.wait_ge(s_rstd, at(i, s_rstd, 2))
                for t in range(NT):
                    e.scalar_tensor_tensor(x_ffn[:, t, :], x_ffn[:, t, :], rstd[:, t:t + 1], mod_row[:, 1, :],
                                           ALU.mult, ALU.add).then_inc(s_xf, 1)

                for l in range(DEPTH):
                    def scaled(t):
                        e.wait_ge(s_rn, at(i, s_rn, l * NT + t + 1))
                        e.wait_ge(s_rsum, at(i, s_rsum, (l * NT + t + 1) * 2))
                        for n in range(2):
                            dst = (q2, k2)[n][:, t, :].rearrange("p (h d) -> p h d", h=H2)
                            r = rnorm[:, t % 2, n * H2:(n + 1) * H2].rearrange("p (h o) -> p h o", o=1)
                            e.tensor_tensor(dst, dst, r.to_broadcast([P, H2, HD2]), ALU.mult).then_inc(s_qn, 1)

                    for t in range(NT):
                        for n in range(2):
                            k = (l * NT + t) * 2 + n
                            e.wait_ge(s_qkv, at(i, s_qkv, (l * NT + t) * 3 + n + 1))
                            if t >= 1:
                                e.wait_ge(s_rsum, at(i, s_rsum, k - 1))
                            src = bank[2 + n + 3 * (t % 2)][:, :].rearrange("p (h a d) -> p h a d", h=H2, a=2)
                            cos = rot[:, l, 2 * n, t, :].rearrange("p (o a d) -> p o a d", o=1, a=2)
                            sin = rot[:, l, 2 * n + 1, t, :].rearrange("p (o a d) -> p o a d", o=1, a=2)
                            to = "p (h a d) -> p h a d"
                            e.wait_ge(s_sq, at(i, s_sq, k + 1))
                            e.tensor_tensor(rot_c[:, n, :].rearrange(to, h=H2, a=2), src,
                                            cos.to_broadcast([P, H2, 2, HD2 // 2]), ALU.mult)
                            e.tensor_tensor(rot_s[:, n, :].rearrange(to, h=H2, a=2), src[:, :, ::-1, :],
                                            sin.to_broadcast([P, H2, 2, HD2 // 2]), ALU.mult).then_inc(s_rt, 1)
                            e.tensor_reduce(ssq[:, t % 2, n * H2:(n + 1) * H2],
                                            sq[:, n, :].rearrange("p (h d) -> p h d", h=H2), AX_X, ALU.add).then_inc(s_vec, own_step())
                        e.wait_ge(s_vec, at(i, s_vec, tally[0]))
                        e.tensor_scalar(ssq[:, t % 2, :], ssq[:, t % 2, :], 1e-24, None, ALU.max).then_inc(s_ss, 1)
                        if t >= 1:
                            scaled(t - 1)
                    scaled(NT - 1)

                    def low2(pair):
                        for n in range(2):
                            for a in range(2):
                                h = 2 * pair + a
                                own, other = slice(64 * a, 64 * a + 64), slice(64 - 64 * a, 128 - 64 * a)
                                e.wait_ge(s_hi2, at(i, s_hi2, (l * H2 // 2 + pair) * 6 + (1 + a if n == 0 else 4 + 2 * a)))
                                high = (q2_stack, k2_high)[n]
                                dst = q2_stack[other, h, :] if n == 0 else k2_low[own, h, :]
                                e.tensor_tensor(dst, bank[n][own, :], high[own, h, :].bitcast(F32),
                                                ALU.subtract).then_inc(s_lo2, 1)

                    def maxima2(h):
                        for n in range(2):
                            k = (l * H2 + h) * 2 + n
                            e.wait_ge(s_s2, at(i, s_s2, k + 1))
                            e.tensor_reduce(neg_max2[:, h % 2, 2 * n:2 * n + 2],
                                            bank[2 + n][:, :].rearrange("p (t k) -> p t k", t=2), AX_X, ALU.max,
                                            negate=True).then_inc(s_m2, 1)
                        e.wait_ge(s_m2, at(i, s_m2, (l * H2 + h + 1) * 2))
                        if h >= G:
                            e.wait_ge(s_t2, at(i, s_t2, (l * H2 + h - G + 1) * 2))
                        for it in range(NT):
                            ins = e.tensor_scalar(diag[:, h % G, it * P:(it + 1) * P], ident_bf[:, :],
                                                  neg_max2[:, h % 2, it:it + 1], None, ALU.mult)
                        ins.then_inc(s_d2, 1)

                    def copy2(pair):
                        k = l * H2 // 2 + pair
                        e.wait_ge(s_pv2, at(i, s_pv2, k + 1))
                        e.tensor_copy(oT2[:, pair, :], bank[6][:, :]).then_inc(s_o2, 1)
                        if pair % 2:
                            e.tensor_copy(denT2[:, pair // 2, :], bank[7][:, :]).then_inc(s_dn, 1)

                    low2(0)
                    for h in range(H2):
                        maxima2(h)
                        if h % 2 == 0 and h // 2 + 1 < H2 // 2:
                            low2(h // 2 + 1)
                        if h >= 3 and h % 2:
                            copy2(h // 2 - 1)
                    copy2(H2 // 2 - 1)
                    for n in range(2):
                        e.wait_ge(s_dT, at(i, s_dT, l * 2 + n + 1))
                        e.reciprocal(rden[:, n, :].rearrange("p (k o) -> p k o", o=1),
                                     bank[n][:, :].rearrange("p (k c) -> p k c", c=32)[:, :, 0:1]).then_inc(s_vec, own_step())
                    e.wait_ge(s_vec, at(i, s_vec, tally[0]))
                    for it in range(NT):
                        e.wait_ge(s_oq2, at(i, s_oq2, l * NT + it + 1))
                        r = rden[:, it // 2, (it % 2) * H2:(it % 2 + 1) * H2].rearrange("p (h o) -> p h o", o=1)
                        e.tensor_tensor(on2[:, it, :].rearrange("p (h d) -> p h d", h=H2),
                                        bank[2 + it][:, :].rearrange("p (h d) -> p h d", h=H2),
                                        r.to_broadcast([P, H2, HD2]), ALU.mult).then_inc(s_on2, 1)
                    for k in (1, 3):
                        e.wait_ge(s_onT2, at(i, s_onT2, l * 4 + k + 1))
                        e.wait_ge(s_onTc2, at(i, s_onTc2, l * 4 + k))
                        e.tensor_copy(onT2[:, k, :], bank[(6, 7, 0, 1)[k]][:, :]).then_inc(s_onTc2, 1)
                    for n in range(2):
                        e.wait_ge(s_p2, at(i, s_p2, l * 2 + n + 1))
                        e.tensor_tensor(x_ffn[:, 2 * n:2 * n + 2, :], bank[2 + n][:, :].rearrange("p (t f) -> p t f", t=2),
                                        x_ffn[:, 2 * n:2 * n + 2, :], ALU.add).then_inc(s_x2, 1)
                    e.wait_ge(s_x2, at(i, s_x2, l * 2 + 2))
                    for t in range(NT):
                        for a in range(2):
                            e.bn_stats(stats[:, t, a, :], x_ffn[:, t, a * P:(a + 1) * P]).then_inc(s_vec, own_step())
                    e.wait_ge(s_vec, at(i, s_vec, tally[0]))
                    e.memset(wait_word[:, :], 0.0)
                    for t in range(NT):
                        e.bn_aggr(mv1[:, t, :], stats[:, t, 0, :]).then_inc(s_vec, own_step())
                    for t in range(NT):
                        ins = e.bn_aggr(mv[:, 1 + t, :], stats[:, t, 1, :])
                    ins.then_inc(s_st, 1)
                    e.wait_ge(s_dshift, at(i, s_dshift, l + 1))
                    moved = bank[0][:, 0:2 * NT].rearrange("p (t c) -> p t c", c=2)
                    mean2, var2, delta, mean, quarter, var = (small[:, n, :] for n in (0, 1, 2, 3, 4, 5))
                    e.tensor_tensor(delta, moved[:, :, 0], mv1[:, :, 0], ALU.subtract).then_inc(s_vec, own_step())
                    e.tensor_tensor(mean2, moved[:, :, 0], mv1[:, :, 0], ALU.add).then_inc(s_vec, own_step())
                    e.tensor_tensor(var2, moved[:, :, 1], mv1[:, :, 1], ALU.add).then_inc(s_vec, own_step())
                    e.wait_ge(s_vec, at(i, s_vec, tally[0]))
                    e.tensor_scalar(mean, mean2, 0.5, None, ALU.mult).then_inc(s_vec, own_step())
                    e.tensor_scalar(var2, var2, 0.5, EPS, ALU.mult, ALU.add).then_inc(s_vec, own_step())
                    e.scalar_tensor_tensor(quarter, delta, 0.25, delta, ALU.mult, ALU.mult).then_inc(s_vec, own_step())
                    e.wait_ge(s_vec, at(i, s_vec, tally[0]))
                    e.tensor_tensor(var, quarter, var2, ALU.add).then_inc(s_var, 1)
                    e.wait_ge(s_rstd, at(i, s_rstd, 3 + l))
                    e.tensor_copy(shift_up[:, 0, 0:NT], rstd[:, :]).then_inc(s_vec, own_step())
                    e.tensor_tensor(shift_up[:, 1, 0:NT], rstd[:, :], mean, ALU.mult).then_inc(s_vec, own_step())
                    e.wait_ge(s_vec, at(i, s_vec, tally[0]))
                    e.tensor_copy(shift_up[:, 1, NT:NT + 1], shift_up[:, 1, 0:1]).then_inc(s_up, 1)
                    for t in range(NT):
                        e.tensor_scalar(y[:, t, 0:P], x_ffn[:, t, 0:P], mean[:, t:t + 1], rstd[:, t:t + 1],
                                        ALU.subtract, ALU.mult).then_inc(s_vec, own_step())
                    e.wait_ge(s_ushift, at(i, s_ushift, l + 1))
                    e.tensor_copy(small[:, 6:8, :], bank[1][:, 0:2 * NT].rearrange("p (c t) -> p c t", c=2)).then_inc(s_vec, own_step())
                    e.wait_ge(s_vec, at(i, s_vec, tally[0]))
                    for t in range(NT):
                        e.tensor_scalar(y[:, t, P:2 * P], x_ffn[:, t, P:2 * P], small[:, 6, t:t + 1], small[:, 7, t:t + 1],
                                        ALU.mult, ALU.subtract).then_inc(s_y, 1)
                    for m in range(HT):
                        r = P if m < HT - 1 else HREST
                        e.wait_ge(s_a, at(i, s_a, l * HT + m + 1))
                        e.wait_ge(s_gl, at(i, s_gl, l * HT + m + 1))
                        e.scalar_tensor_tensor(u[0:r, m, :], bank[3 + 2 * (m % 2)][0:r, :], b1[0:r, l, 0, m:m + 1],
                                               gate[0:r, m % 2, :], ALU.add, ALU.mult).then_inc(s_u, 1)
                    for n in range(2):
                        e.wait_ge(s_f, at(i, s_f, l * 2 + n + 1))
                        e.wait_ge(s_bias, at(i, s_bias, l * 2 + 2))
                        e.tensor_tensor(x_ffn[:, 2 * n:2 * n + 2, :], bank[6 + n][:, :].rearrange("p (t f) -> p t f", t=2),
                                        x_ffn[:, 2 * n:2 * n + 2, :], ALU.add).then_inc(s_x3, 1)
                e.wait_ge(s_gx, at(i, s_gx, 1))
                e.tensor_tensor(y[:, :, :], y[:, :, :], x_res[:, :, :], ALU.add).then_inc(s_res, 1)
                assert tally[0] == VEC, tally[0]

        @block.tensor
        def _(e):
            e.wait_ge(s_const, N_CONST[0])
            e.wait_ge(s_silu, 3)
            for k in range(KD):
                ins = e.transpose(bank[0][:, k * B:(k + 1) * B], silu[:, 1, k * P:(k + 1) * P], ident[0:B, 0:B])
            ins.then_inc(s_silu_t, 1)
            e.wait_ge(s_silu_c, 1)
            for n in range(3):
                for k in range(KD):
                    ins = e.matmul(bank[1 + n][0:B, :], silu_t[:, k, :], wmod[:, k, 512 * n:512 * n + 512],
                                   start=(k == 0), stop=(k == KD - 1))
            ins.then_inc(s_mod, 1)
            e.wait_ge(s_cst_dve, 2)
            e.wait_ge(s_mod_r, 1)

            with e.Fori(0, B) as i:
                for t in range(NT):
                    e.wait_ge(s_y, at(i, s_y, t + 1))
                    for k in range(KD):
                        ins = e.transpose(bank[k][:, t * P:(t + 1) * P], y[:, t, k * P:(k + 1) * P], ident)
                ins.then_inc(s_yT, 1)
                e.wait_ge(s_hT, at(i, s_hT, KD))
                for j in range(4):
                    col = (j % 2) * D + (j // 2) * P
                    for k in range(KD):
                        ins = e.matmul(bank[4 + j][:, :], wqkv1[:, k, col:col + P], hT[:, k, :],
                                       start=(k == 0), stop=(k == KD - 1))
                    ins.then_inc(s_qk, 1)
                for t in range(NT):
                    for k in range(KD):
                        ins = e.matmul(bank[2 + t // 2][:, (t % 2) * D:(t % 2 + 1) * D], hT[:, k, t * P:(t + 1) * P],
                                       wqkv1[:, k, 2 * D:3 * D], start=(k == 0), stop=(k == KD - 1))
                    if t % 2:
                        ins.then_inc(s_v, 1)

                def stack_rows(g, which):
                    m = g * G + which
                    rows = slice(64 * (g % 2) + 32 * (which // 2), 64 * (g % 2) + 32 * (which // 2) + 32)
                    j, n = 2 * (g // 2) + which % 2, which % 2
                    e.wait_ge(s_low, at(i, s_low, 4 if g == 1 else 2 * (g // 2) + 2))
                    if m == 2 or m == 3:
                        e.wait_ge(s_stk, at(i, s_stk, m - 1))
                    elif g:
                        e.wait_ge(s_stk, at(i, s_stk, m))
                        if g == RING and which >= 2:
                            e.wait_ge(s_on1, at(i, s_on1, 1))
                    b = bank[m % 2 if g == 0 else 7]
                    e.matmul(b[:, :], select[rows, 2 * n, :], high1[rows, j, :], start=True, stop=False)
                    e.matmul(b[:, :], select[rows, 2 * n + 1, :], low1[rows, j, :], start=False,
                             stop=True).then_inc(s_sel, 1)

                def scores1(g, h, it):
                    q, k = q_ring[g % RING], k_ring[g % RING]
                    n = (g * G + h) * NT + it
                    if g == 0 and h == 0 and it == 0:
                        e.wait_ge(s_stk, at(i, s_stk, G))
                        e.wait_ge(s_aug, at(i, s_aug, 16 * 2 * RING))
                    elif it == 0:
                        e.wait_ge(s_stk, at(i, s_stk, g * G + h // 2 * 2 + 2))
                    if n >= 2:
                        e.wait_ge(s_m1, at(i, s_m1, n - 1))
                    b = bank[n % 2]
                    e.matmul(b[:, it * P:T], q[0:STACK, h, it * P:(it + 1) * P],
                             k[0:STACK, h, it * P:T], start=True, stop=False, skip_group_check=True)
                    e.matmul(b[:, it * P:(it + 1) * P], ident_bf[:, :], low_bf[:, :], start=False, stop=True,
                             skip_group_check=True).then_inc(s_s1, 1)

                def key_scores1(g, kt, h):
                    q, k, slot = q_ring[g % RING], k_ring[g % RING], (g * G + h) % 8
                    n = (g * NT + NT - 1 - kt) * G + h
                    if n >= 3:
                        e.wait_ge(s_e1, at(i, s_e1, n - 2))
                    elif n == 0:
                        e.wait_ge(s_v1, at(i, s_v1, 2))
                        e.wait_ge(s_low, at(i, s_low, 4))
                    e.wait_ge(s_d1, at(i, s_d1, g * G + h + 1))
                    b, w = bank[2 + n % 3], (kt + 1) * P
                    e.matmul(b[:, 0:w], k[0:STACK, h, kt * P:w], q[0:STACK, h, 0:w],
                             start=True, stop=False, skip_group_check=True)
                    e.matmul(b[:, 0:w], ones_bf[:, :], diag1[slot][:, 0:w], start=False, stop=False,
                             skip_group_check=True)
                    e.matmul(b[:, kt * P:w], ident_bf[:, :], upp_bf[:, :], start=False, stop=True,
                             skip_group_check=True).then_inc(s_t1, 1)

                def values1(g, kt):
                    w = (kt + 1) * P
                    e.wait_ge(s_e1, at(i, s_e1, (g * NT + NT - kt) * G))
                    if kt == NT - 1 and g >= 2:
                        e.wait_ge(s_o1, at(i, s_o1, g - 1))
                    if kt == NT - 1 and g == 0:
                        e.wait_ge(s_v1one, at(i, s_v1one, 1))
                    for h in range(G):
                        ins = e.matmul(bank[5 + g % 2][32 * h:32 * h + 32, 0:w], v1[:, kt, g * G + h, :],
                                       probs1[:, kt % 2, h, 0:w], start=(kt == NT - 1), stop=(kt == 0),
                                       skip_group_check=True)
                    ins.then_inc(s_pv1, 1)

                def back1(g):
                    e.wait_ge(s_o1, at(i, s_o1, g + 1))
                    e.wait_ge(s_stk, at(i, s_stk, min(G * NG1, (g + 3) * G + 2)))
                    if g >= 1:
                        e.wait_ge(s_on1, at(i, s_on1, g))
                    for it in range(NT):
                        ins = e.transpose(bank[7][:, it * P:(it + 1) * P], oT1[:, g % 2, it * P:(it + 1) * P], ident)
                    ins.then_inc(s_oq1, 1)

                for which in range(G):
                    stack_rows(0, which)
                for h in range(G):
                    for it in range(NT):
                        scores1(0, h, it)
                        if it == 1:
                            stack_rows(1, h)
                for g in range(NG1):
                    for step in range(NT):
                        kt = NT - 1 - step
                        for h in range(G):
                            key_scores1(g, kt, h)
                            if g + 1 < NG1:
                                scores1(g + 1, step, h)
                            if h == 1 and g + 2 < NG1:
                                stack_rows(g + 2, step)
                            if h == 1 and step == 1 and g:
                                back1(g - 1)
                        if step:
                            values1(g, kt + 1)
                        elif g:
                            values1(g - 1, 0)
                values1(NG1 - 1, 0)
                back1(NG1 - 1)
                e.wait_ge(s_on1, at(i, s_on1, NG1))
                for t in range(NT):
                    for k in range(KD):
                        ins = e.transpose(bank[k][:, t * P:(t + 1) * P], on1[:, t, k * P:(k + 1) * P], ident)
                ins.then_inc(s_onT1, 1)
                e.wait_ge(s_onTc1, at(i, s_onTc1, KD))
                e.wait_ge(s_wg, at(i, s_wg, 1))
                for t in range(NT):
                    for k in range(KD):
                        ins = e.matmul(bank[2 + t // 2][:, (t % 2) * D:(t % 2 + 1) * D], onT1[:, k, t * P:(t + 1) * P],
                                       wout_g[:, k, :], start=(k == 0), stop=(k == KD - 1))
                    if t % 2:
                        ins.then_inc(s_p1, 1)

                for l in range(DEPTH):
                    for t in range(NT):
                        if l == 0:
                            e.wait_ge(s_xf, at(i, s_xf, t + 1))
                        elif t % 2 == 0:
                            e.wait_ge(s_x3, at(i, s_x3, 2 * l - 1 + t // 2))
                        for k in range(KD):
                            ins = e.transpose(bank[k][:, t * P:(t + 1) * P], x_ffn[:, t, k * P:(k + 1) * P], ident)
                    ins.then_inc(s_xT, 1)
                    e.wait_ge(s_sT, at(i, s_sT, KD * (l + 1)))
                    e.wait_ge(s_zero, at(i, s_zero, l + 1))
                    e.wait_ge(s_lw[0], at(i, s_lw[0], 16 * (l + 1)))
                    for t in range(NT):
                        for n in range(3):
                            b = bank[2 + n + 3 * (t % 2)]
                            if t >= 2:
                                if n < 2:
                                    e.wait_ge(s_rt, at(i, s_rt, (l * NT + t - 2) * 2 + n + 1))
                                else:
                                    e.wait_ge(s_v2, at(i, s_v2, l * NT + t - 1))
                            for k in range(KD):
                                ins = e.matmul(b[:, :], hT[:, k, t * P:(t + 1) * P],
                                               wqkv2[:, k, n * INNER:(n + 1) * INNER], start=(k == 0), stop=(k == KD - 1))
                            ins.then_inc(s_qkv, 1)

                    def turn_pair(pair):
                        for n, src in enumerate((q2, k2)):
                            if pair == 0:
                                e.wait_ge(s_qn, at(i, s_qn, (l + 1) * NT * 2))
                            else:
                                e.wait_ge(s_lo2, at(i, s_lo2, (l * H2 // 2 + pair - 1) * 4 + 2 * n + 2))
                            for t in range(NT):
                                ins = e.transpose(bank[n][:, t * P:(t + 1) * P], src[:, t, pair * P:(pair + 1) * P], ident)
                            ins.then_inc(s_tq, 1)

                    def scores2(h):
                        for n in range(2):
                            k = (l * H2 + h) * 2 + n
                            b = bank[2 + n]
                            e.wait_ge(s_lo2, at(i, s_lo2, (l * H2 // 2 + h // 2 + 1) * 4))
                            if h:
                                e.wait_ge(s_m2, at(i, s_m2, k - 1))
                            e.matmul(b[:, :], ident_bf[:, :], mask_q2[:, 2 * n:2 * n + 4, :], start=True, stop=False,
                                     skip_group_check=True)
                            for it in (2 * n, 2 * n + 1):
                                a = max(it - 1, 0) * P
                                to = (it % 2) * 2 * P + (P if it == 0 else 0)
                                ins = e.matmul(b[:, to:(it % 2 + 1) * 2 * P], q2_stack[:, h, it * P:(it + 1) * P],
                                               k2_high[:, h, a:(it + 1) * P], start=False, stop=(it % 2 == 1),
                                               skip_group_check=True)
                            ins.then_inc(s_s2, 1)

                    def key_scores2(h):
                        e.wait_ge(s_d2, at(i, s_d2, l * H2 + h + 1))
                        if h == 0:
                            e.wait_ge(s_klow0, at(i, s_klow0, 2))
                        for n in range(2):
                            k = (l * H2 + h) * 2 + n
                            w = (512, 384)[n]
                            b = bank[4 + n]
                            if h:
                                e.wait_ge(s_e2, at(i, s_e2, k - 1))
                            e.matmul(b[:, 0:w], ident_bf[:, :], mask_t2[:, 0:w // P, :], start=True, stop=False,
                                     skip_group_check=True)
                            for kt in (2 * n, 2 * n + 1):
                                c = (kt % 2) * 2 * P
                                q = slice(kt * P, min(kt + 2, NT) * P)
                                to = b[:, c:c + q.stop - q.start]
                                for left in (k2_high, k2_low):
                                    e.matmul(to, left[:, h, kt * P:(kt + 1) * P], q2_stack[:, h, q], start=False, stop=False,
                                             skip_group_check=True)
                                ins = e.matmul(to, ones_bf[:, :], diag[:, h % G, q], start=False, stop=(kt % 2 == 1),
                                               skip_group_check=True)
                            ins.then_inc(s_t2, 1)

                    def values2(pair):
                        k = l * H2 // 2 + pair
                        e.wait_ge(s_e2, at(i, s_e2, (l * H2 + 2 * pair + 2) * 2))
                        if pair:
                            e.wait_ge(s_o2, at(i, s_o2, k))
                        if pair == 0:
                            e.wait_ge(s_v2, at(i, s_v2, (l + 1) * NT))
                        if pair == 2:
                            e.wait_ge(s_dn, at(i, s_dn, l * 2 + 1))
                        for kt in range(NT):
                            q = slice(kt * P, min(kt + 2, NT) * P)
                            w = q.stop - q.start
                            for h in (2 * pair, 2 * pair + 1):
                                e.matmul(bank[6][64 * (h % 2):64 * (h % 2) + 64, q], v2[:, kt, h * HD2:(h + 1) * HD2],
                                         probs2[h % 4][:, kt * 256:kt * 256 + w], start=(kt == 0), stop=(kt == NT - 1),
                                         skip_group_check=True)
                            for h in (2 * pair, 2 * pair + 1):
                                c = 32 * (h % 4)
                                ins = e.matmul(bank[7][c:c + 32, q], ones32[:, :],
                                               probs2[h % 4][:, kt * 256:kt * 256 + w], start=(kt == 0), stop=(kt == NT - 1),
                                               skip_group_check=True)
                        ins.then_inc(s_pv2, 1)

                    turn_pair(0)
                    for h in range(H2):
                        scores2(h)
                        if h % 2 == 0 and h // 2 + 1 < H2 // 2:
                            turn_pair(h // 2 + 1)
                        if h >= 1:
                            key_scores2(h - 1)
                        if h >= 3 and h % 2:
                            values2((h - 3) // 2)
                    key_scores2(H2 - 1)
                    values2(H2 // 2 - 1)
                    e.wait_ge(s_dn, at(i, s_dn, l * 2 + 2))
                    for it in range(NT):
                        for a in range(2):
                            c = ((it % 2) * 2 + a) * P
                            ins = e.transpose(bank[it // 2][:, c:c + P], denT2[:, a, it * P:(it + 1) * P], ident)
                        if it % 2:
                            ins.then_inc(s_dT, 1)
                    for it in range(NT):
                        for k in range(H2 // 2):
                            ins = e.transpose(bank[2 + it][:, k * P:(k + 1) * P], oT2[:, k, it * P:(it + 1) * P], ident)
                        ins.then_inc(s_oq2, 1)
                    e.wait_ge(s_on2, at(i, s_on2, (l + 1) * NT))
                    for k in range(4):
                        for it in range(NT):
                            ins = e.transpose(bank[(6, 7, 0, 1)[k]][:, it * P:(it + 1) * P],
                                              on2[:, it, k * P:(k + 1) * P], ident)
                        ins.then_inc(s_onT2, 1)
                    e.wait_ge(s_onTc2, at(i, s_onTc2, (l + 1) * 4))
                    e.wait_ge(s_lw[1], at(i, s_lw[1], 16 * (l + 1)))
                    for t in range(NT):
                        for k in range(4):
                            ins = e.matmul(bank[2 + t // 2][:, (t % 2) * D:(t % 2 + 1) * D], onT2[:, k, t * P:(t + 1) * P],
                                           wo[:, k, :], start=(k == 0), stop=(k == 3))
                        if t % 2:
                            ins.then_inc(s_p2, 1)
                    e.wait_ge(s_st, at(i, s_st, l + 1))
                    moved = bank[0][:, 0:2 * NT]
                    e.matmul(moved, down, mv[:, 1:1 + NT, :], start=True, stop=False)
                    e.matmul(moved, down_wrap, mv[:, 0:NT, :], start=False, stop=True).then_inc(s_dshift, 1)
                    e.wait_ge(s_up, at(i, s_up, l + 1))
                    moved = bank[1][:, 0:2 * NT]
                    e.matmul(moved, up, shift_up[:, :, 0:NT], start=True, stop=False)
                    e.matmul(moved, up_wrap, shift_up[:, :, 1:1 + NT], start=False, stop=True).then_inc(s_ushift, 1)
                    for t in range(NT):
                        e.wait_ge(s_y, at(i, s_y, NT * (l + 1) + t + 1))
                        for k in range(KD):
                            ins = e.transpose(bank[k][:, t * P:(t + 1) * P], y[:, t, k * P:(k + 1) * P], ident)
                    ins.then_inc(s_nT, 1)
                    e.wait_ge(s_nTc, at(i, s_nTc, 3 * (l + 1)))
                    e.wait_ge(s_lw[2], at(i, s_lw[2], 16 * (l + 1)))
                    for m in range(HT):
                        r = P if m < HT - 1 else HREST
                        for half, done in ((1, s_g), (0, s_a)):
                            b = bank[(3, 2)[half] + 2 * (m % 2)]
                            if m >= 2:
                                e.wait_ge(s_u, at(i, s_u, l * HT + m - 1))
                            for k in range(KD):
                                ins = e.matmul(b[0:r, :], w1[:, k, half * HID + m * P:half * HID + m * P + r], hT[:, k, :],
                                               start=(k == 0), stop=(k == KD - 1))
                            ins.then_inc(done, 1)
                    e.wait_ge(s_u, at(i, s_u, (l + 1) * HT))
                    e.wait_ge(s_lw[3], at(i, s_lw[3], 32 * (l + 1)))
                    for t in range(NT):
                        for m in range(HT):
                            r = P if m < HT - 1 else HREST
                            ins = e.matmul(bank[6 + t // 2][:, (t % 2) * D:(t % 2 + 1) * D],
                                           u[0:r, m, t * P:(t + 1) * P], w2[0:r, m, :],
                                           start=(m == 0), stop=(m == HT - 1))
                        if t % 2:
                            ins.then_inc(s_f, 1)


_INS = ['L0_attn_x', 'L0_attn_W_qkv', 'L0_attn_W_out', 'L0_ffn_wqkv', 'L0_ffn_q_scale', 'L0_ffn_k_scale',
        'L0_ffn_wo', 'L0_ffn_ln_g', 'L0_ffn_ln_b', 'L0_ffn_w1', 'L0_ffn_b1', 'L0_ffn_w2', 'L0_ffn_b2', 'L0_c',
        'L0_wmod']


def _constants(tokens, dim):
    import numpy as np

    n = np.arange(P)
    row, col = n[:, None], n[None, :]
    square = np.stack([
        row == col,
        np.where(col < row, NEG, 0.0),
        np.where(col > row, NEG, 0.0),
        np.full((P, P), NEG),
        col == row + 1,
        (row == P - 1) & (col == 0),
        col == row - 1,
        (row == 0) & (col == P - 1),
    ], axis=1).astype(np.float32)
    tiles = tokens // P
    t = np.arange(tokens)
    aug = np.zeros((32, 2, tokens), np.float32)
    aug[0, 0], aug[0, 1] = t % P, 1
    aug[1, 0], aug[1, 1] = 1, -(t % P)
    for a in range(tiles):
        aug[2 + a, 0] = t // P == a
        aug[2 + a, 1] = -P * (t // P - a)
    select = np.zeros((P, 4, 2, 4, 16), np.float32)
    for a in range(P // 32):
        for pair in range(2):
            for r in range(16):
                for which, blocks in enumerate(((0, 2), (1, 3), (0, 1), (2, 3))):
                    select[32 * a + 16 * pair + r, which, pair, blocks, r] = 1
    select = select.reshape(P, 4, P)
    heads = 16
    kscale = np.repeat(0.25 / np.array(slopes(heads)), dim // heads)[None, :].astype(np.float32)
    d, window = 64, 128
    f = np.float32
    half = np.arange(0, d, 2, dtype=f)
    inv = f(1.0) / np.power(f(10000.0), half / f(d))
    tt = np.arange(tokens, dtype=f)
    freq = tt[:, None] * inv[None, :]
    freq = np.concatenate([freq, freq], -1)
    base = (half + f(0.4 * d)) / f(1.4 * d)
    power = (tt - f(tokens // 2)) / f(window // 2)
    scale = np.power(base[None, :], power[:, None])
    scale = np.concatenate([scale, scale], -1)
    sign = np.where(np.arange(d) < d // 2, f(-1), f(1))
    cos, sin = np.cos(freq), np.sin(freq) * sign
    rot = np.stack([cos * scale, sin * scale, cos / scale, sin / scale]).astype(np.float32)
    rot = rot.reshape(4, tiles, P, d).transpose(2, 0, 1, 3)
    return {"square": square, "aug": aug, "select": select, "rot": np.ascontiguousarray(rot), "kscale": kscale}


def kernel(**inputs):
    import numpy as _np
    import concourse.bacc as _bacc
    from concourse import mybir as _mybir
    from concourse.bass_utils import run_bass_kernel_spmd as _run

    nc = _bacc.Bacc("TRN2", target_bir_lowering=False, num_devices=1)
    arrays, args = {}, []
    batch, tokens, dim = inputs['L0_attn_x'].shape
    data = [(n, inputs[n]) for n in _INS] + list(_constants(tokens, dim).items())
    for name, value in data:
        a = _np.ascontiguousarray(value)
        arrays[f"in_{name}_dram"] = a
        args.append(nc.dram_tensor(f"in_{name}_dram", a.shape, _mybir.dt.from_np(a.dtype), kind="ExternalInput").ap())
    out = nc.dram_tensor("out_0_dram", (batch, tokens, dim), _mybir.dt.float32, kind="ExternalOutput").ap()
    adaln_block(nc, *args, out)
    r = _run(nc, [arrays], core_ids=[0])
    return r.results[0]["out_0_dram"]
```

```python
from contextlib import ExitStack

import concourse.bass as bass
from concourse import mybir

ALU = mybir.AluOpType
ACT = mybir.ActivationFunctionType
AX_X = mybir.AxisListType.X
F32 = mybir.dt.float32
F32R = mybir.dt.float32r
BF16 = mybir.dt.bfloat16

P = 128
NEG = -1e30
EPS = 1e-5


def slopes(heads):
    start = 2.0 ** (-8.0 / heads)
    return [start ** (h + 1) for h in range(heads)]


def adaln_block(nc, x_in, wqkv1_in, wout_in, wqkv2_in, qs_in, ks_in, wo_in, lng_in, lnb_in,
                w1_in, b1_in, w2_in, b2_in, c_in, wmod_in, square_in, aug_in, select_in, rot_in, kscale_in, out):
    B, T, D = x_in.shape
    NT = T // P
    KD = D // P
    H1 = 16
    HD1 = D // H1
    DEPTH, _, W3 = wqkv2_in.shape
    INNER = W3 // 3
    HD2 = qs_in.shape[1]
    H2 = INNER // HD2
    HID = w2_in.shape[1]
    HT = (HID + P - 1) // P
    HREST = HID - (HT - 1) * P
    QK_SCALE = 8.0
    G = 4
    NG1 = H1 // G
    SLOPE = slopes(H1)
    STACK = 64 + aug_in.shape[0]
    RING = 3
    POS_ROW = 64

    with ExitStack() as ctx:
        def sb(name, shape, dt=F32):
            return ctx.enter_context(nc.sbuf_tensor(name, shape, dt))

        per_batch, first = {}, {}

        def sem(name, per=0, before=0):
            s = ctx.enter_context(nc.semaphore(name))
            per_batch[id(s)], first[id(s)] = per, before
            return s

        bank = [ctx.enter_context(nc.psum_tensor(f"bank{n}", [P, 512], F32)) for n in range(8)]

        square = sb("square", [P, 8, P])
        ident = square[:, 0, :]
        down, down_wrap, up, up_wrap = (square[:, n, :] for n in range(4, 8))
        ident_bf = sb("ident_bf", [P, P], BF16)
        ones_bf = sb("ones_bf", [P, P], BF16)
        low_bf = sb("low_bf", [P, P], BF16)
        upp_bf = sb("upp_bf", [P, P], BF16)
        mask_q2 = sb("mask_q2", [P, 6, P], BF16)
        mask_t2 = sb("mask_t2", [P, 4, P], BF16)
        ones32 = sb("ones32", [P, 32])
        aug = sb("aug", [P, 2, T], F32R)
        select = sb("select", [P, 4, P], F32R)
        half_power = sb("half_power", [P, 2 * H2])
        rot = sb("rot", [P, DEPTH, 4, NT, HD2])

        wqkv1 = sb("wqkv1", [P, KD, 3 * D])
        wout = sb("wout", [P, KD, D])
        wout_g = sb("wout_g", [P, KD, D])
        wqkv2 = sb("wqkv2", [P, KD, W3])
        wo = sb("wo", [P, INNER // P, D])
        w1 = sb("w1", [P, KD, 2 * HID])
        w2 = sb("w2", [P, HT, D])
        b1 = sb("b1", [P, DEPTH, 2, HT])
        b2 = sb("b2", [P, DEPTH, D])
        lng = sb("lng", [P, DEPTH, KD])
        lnb = sb("lnb", [P, DEPTH, KD])

        mod_col = sb("mod_col", [P, 2, KD])
        mod_row = sb("mod_row", [P, 4, D])
        silu_t = sb("silu_t", [P, KD, B])
        mod_dram = nc.dram_tensor("mod_scratch", [B, 6 * D], F32).ap()

        x_res = sb("x_res", [P, NT, D])
        x_ffn = sb("x_ffn", [P, NT, D])
        y = sb("y", [P, NT, D])
        hT = sb("hT", [P, KD, T])
        stats = sb("stats", [P, NT, 2, 6])
        mv = sb("mv", [P, 5, 2])
        wait_word = sb("wait_word", [P, 1])
        zero_one = sb("zero_one", [P, 2])
        mv1 = sb("mv1", [P, NT, 2])
        small = sb("small", [P, 8, NT])
        shift_up = sb("shift_up", [P, 2, 5])
        rstd = sb("rstd", [P, NT])
        neg_max = sb("neg_max", [P, 2, G, NT])
        neg_max2 = sb("neg_max2", [P, 2, NT])
        diag = sb("diag", [P, G, T], BF16)
        ssq = sb("ssq", [P, 2, 2 * H2])
        rnorm = sb("rnorm", [P, 2, 2 * H2])
        rden = sb("rden", [P, 2, NT * G])

        stack = sb("stack", [P, (8 + 8 * RING) * T], F32R)
        high1 = stack[:, 0:4 * T].rearrange("p (j t) -> p j t", j=4)
        low1 = stack[:, 4 * T:8 * T].rearrange("p (j t) -> p j t", j=4)
        q_ring, k_ring = ([stack[:, (8 + 8 * g + 4 * n) * T:(12 + 8 * g + 4 * n) * T].rearrange("p (h t) -> p h t", h=G)
                           for g in range(RING)] for n in range(2))
        q2_stack = stack[:, 0:8 * T].rearrange("p (h t) -> p h t", h=8)
        k2_high = stack[:, 8 * T:16 * T].rearrange("p (h t) -> p h t", h=8)
        k2_low = stack[:, 16 * T:24 * T].rearrange("p (h t) -> p h t", h=8)

        scratch = sb("scratch", [P, 26 * T])

        def part(a, n, pattern, **kw):
            return scratch[:, a * T:(a + n) * T].rearrange(pattern, **kw)

        v1 = part(0, 4, "p (t h c) -> p t h c", t=NT, h=H1)
        probs1 = part(4, 8, "p (s h q) -> p s h q", s=2, h=G)
        oT1 = part(12, 2, "p (s q) -> p s q", s=2)
        on1 = part(14, 2, "p (t f) -> p t f", t=NT)
        onT1 = part(16, 2, "p (k q) -> p k q", k=KD)
        more_diag = part(18, 2, "p (s q) -> p s q", s=2).bitcast(BF16).rearrange("p s (a q) -> p (s a) q", a=2)
        diag1 = [diag[:, n, :] for n in range(G)] + [more_diag[:, n, :] for n in range(G)]
        q2 = part(0, 4, "p (t f) -> p t f", t=NT)
        k2 = part(4, 4, "p (t f) -> p t f", t=NT)
        rot_c = part(8, 2, "p (s f) -> p s f", s=2)
        rot_s = part(10, 2, "p (s f) -> p s f", s=2)
        sq = part(12, 2, "p (s f) -> p s f", s=2)
        v2 = part(14, 4, "p (t f) -> p t f", t=NT)
        probs2 = [part(a, 2, "p (s q) -> p (s q)", s=1) for a in (8, 10, 12, 18)]
        oT2 = part(20, 4, "p (k q) -> p k q", k=H2 // 2)
        denT2 = part(24, 2, "p (k q) -> p k q", k=H2 // G)
        on2 = q2
        onT2 = part(4, 4, "p (k q) -> p k q", k=H2 // 2)
        gate = part(0, 2, "p (s q) -> p s q", s=2)
        u = part(2, HT, "p (m q) -> p m q", m=HT)
        wmod = scratch[:, 0:KD * 6 * D].rearrange("p (k n) -> p k n", k=KD)
        mod_rows = scratch[0:B, 12 * D:18 * D]
        mod_abs = scratch[0:B, 18 * D:19 * D]
        mod_sign = scratch[0:B, 19 * D:20 * D]
        setup_select = part(12, 1, "p (s c) -> p s c", s=4)
        setup_aug = part(13, 2, "p (s t) -> p s t", s=2)
        silu = scratch[0:B, 20 * D:23 * D].rearrange("p (a f) -> p a f", a=3)

        s_const = sem("const_loaded")
        s_cst_dve = sem("const_made")
        s_silu = sem("silu_steps")
        s_silu_e = sem("silu_exp")
        s_silu_t = sem("silu_transposed")
        s_silu_c = sem("silu_copied")
        s_mod = sem("mod_product")
        s_mod_r = sem("mod_rows_ready")
        s_mod_st = sem("mod_stored")
        VEC = 98
        POOL_SUMS = 2 * NT - NT // 2
        s_vec = sem("vector_step", VEC)
        s_x = sem("x_loaded", 16)
        s_xn = sem("next_x_loaded", 16, before=16)
        s_modc = sem("mod_columns_loaded", 32, before=32)
        s_modr = sem("mod_rows_loaded", 16)
        s_var = sem("variance_ready", 4, before=1)
        s_rstd = sem("rstd_ready", 4, before=1)
        s_yn = sem("first_norm_ready", NT, before=NT)
        s_y = sem("normed_ready", 2 * NT)
        s_yT = sem("normed_transposed", 1)
        s_hT = sem("features_ready", KD)
        s_qk = sem("qk_projected", 4)
        s_v = sem("v_projected", 2)
        s_high = sem("high_part_ready", 4)
        s_low = sem("low_part_ready", 4)
        s_v1 = sem("v_copied", 2)
        s_v1one = sem("v_ones_set", 1)
        s_aug = sem("position_rows_loaded", 16 * 2 * RING)
        s_sel = sem("stack_rows_ready", NG1 * G)
        s_stk = sem("stack_rows_copied", NG1 * G)
        s_s1 = sem("scores_ready", H1 * NT)
        s_m1 = sem("maximum_taken", H1 * NT)
        s_d1 = sem("diagonal_ready", H1)
        s_t1 = sem("key_scores_ready", H1 * NT)
        s_e1 = sem("probs_ready", H1 * NT)
        s_pv1 = sem("values_summed", H1)
        s_o1 = sem("heads_copied", NG1)
        s_oq1 = sem("heads_transposed", NG1)
        s_on1 = sem("heads_normed", NG1)
        s_onT1 = sem("attn_transposed", 1)
        s_onTc1 = sem("attn_features_ready", KD)
        s_wg = sem("gated_weights_ready", 1)
        s_p1 = sem("attn_out_ready", 2)
        s_x1 = sem("residual_ready", 2)
        s_xf = sem("ffn_input_ready", NT)
        s_xT = sem("stream_transposed", DEPTH)
        s_zero = sem("first_column_zeroed", DEPTH)
        s_sT = sem("first_features_ready", DEPTH)
        s_sTd = sem("shifted_features_ready", DEPTH)
        s_qk2 = sem("qk2_ready", DEPTH * 2 * NT)
        s_vp2 = sem("v2_ready", DEPTH * NT)
        s_sq = sem("squares_ready", DEPTH * 2 * NT)
        s_rt = sem("rotated_parts_ready", DEPTH * 2 * NT)
        s_ss = sem("square_sums_ready", DEPTH * 2 * NT)
        s_rsum = sem("rotated_sum_ready", DEPTH * POOL_SUMS)
        s_rn = sem("inverse_norm_ready", DEPTH * 2 * NT)
        s_qn = sem("heads_scaled", DEPTH * 2 * NT)
        s_v2 = sem("v2_copied", DEPTH * NT)
        s_tq = sem("pair_transposed", DEPTH * H2)
        s_hi2 = sem("head_high_ready", DEPTH * 3 * H2)
        s_lo2 = sem("head_low_ready", DEPTH * 2 * H2)
        s_klow0 = sem("low_stacks_zeroed", 2)
        s_s2 = sem("local_scores_ready", DEPTH * 2 * H2)
        s_m2 = sem("local_maximum_taken", DEPTH * 2 * H2)
        s_d2 = sem("local_diagonal_ready", DEPTH * H2)
        s_t2 = sem("local_key_scores_ready", DEPTH * 2 * H2)
        s_e2 = sem("local_probs_ready", DEPTH * 2 * H2)
        s_pv2 = sem("local_values_summed", DEPTH * H2 // 2)
        s_o2 = sem("local_heads_copied", DEPTH * H2 // 2)
        s_dn = sem("denominators_copied", DEPTH * 2)
        s_dT = sem("denominators_transposed", DEPTH * 2)
        s_oq2 = sem("local_heads_transposed", DEPTH * NT)
        s_on2 = sem("local_heads_normed", DEPTH * NT)
        s_onT2 = sem("local_attn_transposed", DEPTH * 4)
        s_onTc2 = sem("local_attn_features_ready", DEPTH * 2)
        s_onTd2 = sem("local_attn_features_too", DEPTH * 2)
        s_p2 = sem("local_attn_out_ready", DEPTH * 2)
        s_x2 = sem("stream_ready", DEPTH * 2)
        s_st = sem("half_stats_ready", DEPTH)
        s_dshift = sem("stats_shifted", DEPTH)
        s_up = sem("up_stats_ready", DEPTH)
        s_ushift = sem("up_stats_shifted", DEPTH)
        s_nT = sem("norm_transposed", DEPTH)
        s_nTc = sem("first_norm_features_ready", DEPTH)
        s_nTd = sem("shifted_norm_features_ready", DEPTH * 2)
        s_g = sem("gate_product_ready", DEPTH * HT)
        s_a = sem("value_product_ready", DEPTH * HT)
        s_gl = sem("gelu_ready", DEPTH * HT)
        s_u = sem("hidden_ready", DEPTH * HT)
        s_bias = sem("stream_biased", DEPTH * 2)
        s_f = sem("ffn_out_ready", DEPTH * 2)
        s_x3 = sem("layer_done", DEPTH * 2, before=1)
        s_gx = sem("gated_stream_ready", 1, before=1)
        s_res = sem("result_ready", 1, before=1)
        s_out = sem("result_stored", 16, before=16)
        s_lw = [sem(f"layer_weights_{n}_loaded", 16 * DEPTH * (2 if n == 3 else 1)) for n in range(4)]

        def at(i, s, k):
            assert k + first[id(s)] >= 1
            return i * per_batch[id(s)] + k + first[id(s)]

        PROJECTIONS = []
        SPREAD = [(2, 2, 1, 1), (1, 1, 1, 1), (1, 1, 1, 1), (1, 1, 0, 0)]
        assert sum(map(sum, SPREAD)) == G * NT
        for t in range(NT):
            PROJECTIONS.append((t, "qk"))
            if t >= 1:
                PROJECTIONS.append((t - 1, "v"))
        PROJECTIONS.append((NT - 1, "v"))

        def on_pool(t, n):
            return not (t % 2 and n)

        def pool_sums(l, t, n):
            return l * POOL_SUMS + sum(on_pool(a, b) for a in range(NT) for b in range(2) if (a, b) <= (t, n))

        N_CONST = [0]
        block = ctx.enter_context(nc.Block())

        def load_layer(e, l, what):
            if what == 0:
                e.dma_start(wqkv2[:, :, :], wqkv2_in[l].rearrange("(k p) n -> p k n", p=P)).then_inc(s_lw[0], 16)
            if what == 1:
                e.dma_start(wo[:, :, :], wo_in[l].rearrange("(k p) n -> p k n", p=P)).then_inc(s_lw[1], 16)
            if what == 2:
                e.dma_start(w1[:, :, :], w1_in[l].rearrange("(k p) n -> p k n", p=P)).then_inc(s_lw[2], 16)
            if what == 3:
                e.dma_start(w2[:, 0:HT - 1, :], w2_in[l, 0:(HT - 1) * P, :].rearrange("(k p) n -> p k n", p=P)).then_inc(s_lw[3], 16)
                e.dma_start(w2[0:HREST, HT - 1, :], w2_in[l, (HT - 1) * P:HID, :]).then_inc(s_lw[3], 16)

        @block.sync
        def _(e):
            def c(dst, src, thin=False):
                e.dma_start(dst, src, allow_slow_non_contiguous=thin).then_inc(s_const, 16)
                N_CONST[0] += 16

            c(silu[:, 0, :], c_in)
            c(square[:, :, :], square_in)
            c(wmod, wmod_in.rearrange("(k p) n -> p k n", p=P))
            c(setup_select, select_in)
            c(setup_aug[POS_ROW:STACK, :, :], aug_in)
            c(wqkv1[:, :, :], wqkv1_in.rearrange("(k p) n -> p k n", p=P))
            c(wout[:, :, :], wout_in.rearrange("(k p) n -> p k n", p=P))
            c(x_res[:, 0, :], kscale_in.to_broadcast([P, D]))
            for l in range(DEPTH):
                c(rot[:, l, :, :, :], rot_in)
                c(b2[:, l, :], b2_in[l:l + 1, :].to_broadcast([P, D]))
                c(lng[:, l, :], lng_in[l].rearrange("(k p) -> p k", p=P), thin=True)
                c(lnb[:, l, :], lnb_in[l].rearrange("(k p) -> p k", p=P), thin=True)
                c(x_ffn[:, l, 0:HD2], qs_in[l:l + 1, :].to_broadcast([P, HD2]))
                c(x_ffn[:, l, HD2:2 * HD2], ks_in[l:l + 1, :].to_broadcast([P, HD2]))
                for half in range(2):
                    c(b1[:, l, half, 0:HT - 1],
                      b1_in[l, half * HID:half * HID + (HT - 1) * P].rearrange("(m p) -> p m", p=P), thin=True)
                    c(b1[0:HREST, l, half, HT - 1:HT],
                      b1_in[l, half * HID + (HT - 1) * P:(half + 1) * HID].rearrange("(p m) -> p m", m=1), thin=True)
            for what in range(4):
                load_layer(e, 0, what)
            e.wait_ge(s_mod_r, 1)
            e.dma_start(mod_dram, mod_rows[:, :]).then_inc(s_mod_st, 16)
            e.wait_ge(s_mod_st, 16)

            e.dma_start(y[:, :, :], x_in[0].rearrange("(t p) f -> p t f", p=P)).then_inc(s_xn, 16)
            for n in range(2):
                e.dma_start(mod_col[:, n, :], mod_dram[0, n * D:(n + 1) * D].rearrange("(k p) -> p k", p=P),
                            allow_slow_non_contiguous=True).then_inc(s_modc, 16)

            with e.Fori(0, B) as i:
                for g in range(RING):
                    for n, ring in enumerate((q_ring, k_ring)):
                        e.dma_start(ring[g][POS_ROW:STACK, :, :].bitcast(F32),
                                    aug[POS_ROW:STACK, n:n + 1, :].bitcast(F32).to_broadcast([STACK - POS_ROW, G, T])).then_inc(s_aug, 16)
                e.wait_ge(s_gx, at(i, s_gx, 0))
                e.dma_start(mod_row[:, :, :].rearrange("p a f -> p (a f)"),
                            mod_dram[bass.ds(i, 1), 2 * D:6 * D].to_broadcast([P, 4 * D])).then_inc(s_modr, 16)
                e.wait_ge(s_out, at(i, s_out, 0))
                e.dma_start(x_res[:, :, :], x_in[bass.ds(i, 1)].rearrange("o (t p) f -> p (o t) f", p=P)).then_inc(s_x, 16)
                for l in range(DEPTH):
                    nxt = (l + 1) % DEPTH
                    e.wait_ge(s_vp2, at(i, s_vp2, NT * (l + 1)))
                    load_layer(e, nxt, 0)
                    e.wait_ge(s_p2, at(i, s_p2, 2 * (l + 1)))
                    load_layer(e, nxt, 1)
                    if l == DEPTH - 1:
                        e.wait_ge(s_nT, at(i, s_nT, DEPTH))
                        e.dma_start(y[:, :, :], x_in[bass.ds((i + 1) % B, 1)].rearrange("o (t p) f -> p (o t) f", p=P)
                                    ).then_inc(s_xn, 16)
                        for n in range(2):
                            e.dma_start(mod_col[:, n, :],
                                        mod_dram[bass.ds((i + 1) % B, 1), n * D:(n + 1) * D].rearrange("o (k p) -> p (o k)", p=P),
                                        allow_slow_non_contiguous=True).then_inc(s_modc, 16)
                    e.wait_ge(s_a, at(i, s_a, HT * (l + 1)))
                    load_layer(e, nxt, 2)
                    e.wait_ge(s_f, at(i, s_f, 2 * (l + 1)))
                    load_layer(e, nxt, 3)
                e.wait_ge(s_res, at(i, s_res, 1))
                e.dma_start(out[bass.ds(i, 1)].rearrange("o (t p) f -> p (o t) f", p=P), x_res[:, :, :]).then_inc(s_out, 16)
            e.wait_ge(s_out, 16 * B + 16)
            e.wait_ge(s_xn, 16 * B + 16)
            e.wait_ge(s_modc, 32 * B + 32)
            for n in range(4):
                e.wait_ge(s_lw[n], per_batch[id(s_lw[n])] * B + (32 if n == 3 else 16))

        @block.gpsimd
        def _(e):
            e.memset(half_power[:, :], -0.5).then_inc(s_cst_dve, 1)
            e.memset(ones32[:, :], 1.0)
            e.memset(zero_one[:, 0:1], 0.0)
            e.memset(zero_one[:, 1:2], 1.0)
            e.memset(mv[:, 0, :], 0.0)
            e.memset(shift_up[:, 0, NT:NT + 1], 0.0)
            e.memset(ones_bf[:, :], 1.0).then_inc(s_cst_dve, 1)
            e.wait_ge(s_const, N_CONST[0])
            e.wait_ge(s_cst_dve, 2)

            def power(dst, src, width):
                return e.tensor_tensor(dst, src, half_power[:, 0:width], ALU.pow)

            def fill(dst, word):
                n, a, b = dst.shape
                word = word.rearrange("p (a b) -> p a b", a=1).to_broadcast([n, a, b])
                return e.tensor_tensor(dst, word, word, ALU.mult)

            def diagonal(dst, values):
                return e.tensor_tensor(dst.rearrange("p (t c) -> p t c", t=NT),
                                       square[:, 0:1, :].to_broadcast([P, NT, P]),
                                       values.rearrange("p (t o) -> p t o", o=1).to_broadcast([P, NT, P]), ALU.mult)

            e.wait_ge(s_var, 1)
            power(rstd[:, :], small[:, 0, :], NT).then_inc(s_rstd, 1)
            e.wait_ge(s_mod_r, 1)

            with e.Fori(0, B) as i:
                for t in range(NT):
                    ins = fill(v1[:, t, :, HD1:2 * HD1], zero_one[:, 1:2])
                ins.then_inc(s_v1one, 1)
                e.wait_ge(s_modr, at(i, s_modr, 16))
                e.tensor_tensor(wout_g[:, :, :], wout[:, :, :],
                                mod_row[:, 0:1, :].to_broadcast([P, KD, D]), ALU.mult).then_inc(s_wg, 1)
                for g in range(NG1):
                    for h in range(G):
                        e.wait_ge(s_m1, at(i, s_m1, (g * G + h + 1) * NT))
                        if g >= 2:
                            e.wait_ge(s_t1, at(i, s_t1, G * NT * (g - 1)))
                        diagonal(diag1[(g * G + h) % 8], neg_max[:, g % 2, h, :]).then_inc(s_d1, 1)
                e.wait_ge(s_var, at(i, s_var, 1))
                power(rstd[:, :], small[:, 0, :], NT).then_inc(s_rstd, 1)
                e.wait_ge(s_v, at(i, s_v, 2))
                fill(hT[:, 1:2, 0:1], zero_one[:, 0:1]).then_inc(s_zero, 1)
                for a in range(2):
                    zero = slice(64 - 64 * a, 128 - 64 * a)
                    if a:
                        e.wait_ge(s_klow0, at(i, s_klow0, a))
                    else:
                        e.wait_ge(s_zero, at(i, s_zero, 1))
                    fill(k2_low[zero, a::2, :], zero_one[zero, 0:1]).then_inc(s_klow0, 1)
                e.wait_ge(s_klow0, at(i, s_klow0, 2))
                for l in range(DEPTH):
                    if l:
                        e.wait_ge(s_xT, at(i, s_xT, l + 1))
                        fill(hT[:, 1:2, 0:1], zero_one[:, 0:1]).then_inc(s_zero, 1)
                    for t in range(NT):
                        for n in range(2):
                            k = (l * NT + t) * 2 + n
                            dst = (q2, k2)[n]
                            if on_pool(t, n):
                                e.wait_ge(s_rt, at(i, s_rt, k + 1))
                                e.tensor_tensor(dst[:, t, :], rot_c[:, n, :], rot_s[:, n, :], ALU.add).then_inc(s_rsum, 1)
                            e.wait_ge(s_ss, at(i, s_ss, k + 1))
                            heads = slice(n * H2, (n + 1) * H2)
                            power(rnorm[:, t % 2, heads], ssq[:, t % 2, heads], H2).then_inc(s_rn, 1)
                    for h in range(H2):
                        e.wait_ge(s_m2, at(i, s_m2, (l * H2 + h + 1) * 2))
                        if h >= G:
                            e.wait_ge(s_t2, at(i, s_t2, (l * H2 + h - G + 1) * 2))
                        diagonal(diag[:, h % G, :], neg_max2[:, h % 2, :]).then_inc(s_d2, 1)
                    e.wait_ge(s_var, at(i, s_var, 2 + l))
                    power(rstd[:, :], small[:, 5, :], NT).then_inc(s_rstd, 1)
                    e.wait_ge(s_y, at(i, s_y, NT * (l + 1)))
                    for n in range(2):
                        e.tensor_tensor(x_ffn[:, 2 * n:2 * n + 2, :], x_ffn[:, 2 * n:2 * n + 2, :],
                                        b2[:, l:l + 1, :].to_broadcast([P, 2, D]), ALU.add).then_inc(s_bias, 1)
                e.wait_ge(s_var, at(i, s_var, 4))
                power(rstd[:, :], small[:, 0, :], NT).then_inc(s_rstd, 1)
                e.wait_ge(s_x3, at(i, s_x3, 2 * DEPTH))
                e.tensor_tensor(x_ffn[:, :, :], x_ffn[:, :, :],
                                mod_row[:, 3:4, :].to_broadcast([P, NT, D]), ALU.mult).then_inc(s_gx, 1)

        @block.scalar
        def _(e):
            e.wait_ge(s_const, N_CONST[0])
            e.activation(silu[:, 1, :], silu[:, 0, :], ACT.Exp, scale=-1.0).then_inc(s_silu_e, 1)

            with e.Fori(0, B) as i:
                e.wait_ge(s_yT, at(i, s_yT, 1))
                e.wait_ge(s_modc, at(i, s_modc, 0))
                for k in range(KD):
                    e.activation(hT[:, k, :], bank[k][:, :], ACT.Identity, scale=mod_col[:, 1, k:k + 1],
                                 bias=mod_col[:, 0, k:k + 1]).then_inc(s_hT, 1)
                def stack_rows(g, which):
                    m = g * G + which
                    e.wait_ge(s_sel, at(i, s_sel, m + 1))
                    if g >= RING:
                        e.wait_ge(s_t1, at(i, s_t1, G * NT * (g - RING + 1)))
                    b = bank[m % 2 if g == 0 else 7]
                    for a in range(2):
                        ins = e.activation((q_ring, k_ring)[which % 2][g % RING][0:POS_ROW, 2 * (which // 2) + a, :],
                                           b[64 * a:64 * a + 64, :], ACT.Copy)
                    ins.then_inc(s_stk, 1)

                def high_part(j):
                    e.wait_ge(s_qk, at(i, s_qk, j + 1))
                    e.activation(high1[:, j, :], bank[4 + j][:, :], ACT.Copy).then_inc(s_high, 1)

                high_part(0)
                high_part(1)
                for n in range(2):
                    e.wait_ge(s_v, at(i, s_v, n + 1))
                    e.activation(v1[:, 2 * n:2 * n + 2, :, 0:HD1],
                                 bank[2 + n][:, :].rearrange("p (t h c) -> p t h c", t=2, h=H1), ACT.Copy).then_inc(s_v1, 1)
                for j in (2, 3):
                    stack_rows(0, 2 * j - 4)
                    stack_rows(0, 2 * j - 3)
                    high_part(j)
                for which in range(G):
                    stack_rows(1, which)
                n = 0
                for g in range(NG1):
                    for step, kt in enumerate(reversed(range(NT))):
                        if g * NT + step >= 2:
                            e.wait_ge(s_pv1, at(i, s_pv1, g * NT + step - 1))
                        for h in range(G):
                            n += 1
                            e.wait_ge(s_t1, at(i, s_t1, n))
                            w = (kt + 1) * P
                            e.activation(probs1[:, kt % 2, h, 0:w], bank[2 + (n - 1) % 2][:, 0:w], ACT.Exp,
                                         scale=SLOPE[g * G + h]).then_inc(s_e1, 1)
                            if h == 1 and g + 2 < NG1:
                                stack_rows(g + 2, step)
                e.wait_ge(s_onT1, at(i, s_onT1, 1))
                for k in range(KD):
                    e.activation(onT1[:, k, :], bank[k][:, :], ACT.Copy).then_inc(s_onTc1, 1)

                for l in range(DEPTH):
                    e.wait_ge(s_xT, at(i, s_xT, l + 1))
                    e.activation(hT[:, 0, :], bank[0][:, :], ACT.Copy).then_inc(s_sT, 1)
                    for t, what in PROJECTIONS:
                        if what == "v":
                            e.wait_ge(s_vp2, at(i, s_vp2, l * NT + t + 1))
                            e.activation(v2[:, t, :], bank[4 + 3 * (t % 2)][:, :], ACT.Copy).then_inc(s_v2, 1)
                            continue
                        for n in range(2):
                            k = (l * NT + t) * 2 + n
                            if t >= 1:
                                e.wait_ge(s_ss, at(i, s_ss, k - 1))
                            e.wait_ge(s_qk2, at(i, s_qk2, k + 1))
                            e.activation(sq[:, n, :], bank[2 + n + 3 * (t % 2)][:, :], ACT.Square).then_inc(s_sq, 1)

                    def high2(pair):
                        for n in range(2):
                            e.wait_ge(s_tq, at(i, s_tq, (l * H2 // 2 + pair) * 2 + n + 1))
                            for a in range(2):
                                src = bank[n][64 * a:64 * a + 64, :]
                                own, other = slice(64 * a, 64 * a + 64), slice(64 - 64 * a, 128 - 64 * a)
                                dst = (q2_stack, k2_high)[n]
                                e.activation(dst[own, 2 * pair + a, :], src, ACT.Copy).then_inc(s_hi2, 1)
                                if n == 1:
                                    e.activation(dst[other, 2 * pair + a, :], src, ACT.Copy).then_inc(s_hi2, 1)

                    high2(0)
                    for h in range(H2 + 1):
                        if h >= 1:
                            g = h - 1
                            if g >= 4:
                                e.wait_ge(s_pv2, at(i, s_pv2, l * H2 // 2 + (g - 4) // 2 + 1))
                            for n in range(2):
                                e.wait_ge(s_t2, at(i, s_t2, (l * H2 + g) * 2 + n + 1))
                                w = (512, 384)[n]
                                e.activation(probs2[g % 4][:, 512 * n:512 * n + w], bank[4 + n][:, 0:w],
                                             ACT.Exp).then_inc(s_e2, 1)
                        if h % 2 == 0 and h // 2 + 1 < H2 // 2:
                            high2(h // 2 + 1)
                    for k in (0, 2):
                        e.wait_ge(s_onT2, at(i, s_onT2, l * 4 + k + 1))
                        e.activation(onT2[:, k, :], bank[(6, 7, 0, 1)[k]][:, :], ACT.Copy).then_inc(s_onTc2, 1)
                    e.wait_ge(s_nT, at(i, s_nT, l + 1))
                    e.activation(hT[:, 0, :], bank[0][:, :], ACT.Identity, scale=lng[:, l, 0:1],
                                 bias=lnb[:, l, 0:1]).then_inc(s_nTc, 1)
                    for m in range(HT):
                        r = P if m < HT - 1 else HREST
                        e.wait_ge(s_g, at(i, s_g, l * HT + m + 1))
                        if m >= 2:
                            e.wait_ge(s_u, at(i, s_u, l * HT + m - 1))
                        e.activation(gate[0:r, m % 2, :], bank[2 + 2 * (m % 2)][0:r, :], ACT.Gelu,
                                     bias=b1[0:r, l, 1, m:m + 1]).then_inc(s_gl, 1)

        @block.vector
        def _(e):
            e.wait_ge(s_const, N_CONST[0])
            chain = [0]

            def setup_step():
                chain[0] += 1
                return 1

            e.wait_ge(s_silu_e, 1)
            e.tensor_scalar(silu[:, 1, :], silu[:, 1, :], 1.0, None, ALU.add).then_inc(s_silu, setup_step())
            e.wait_ge(s_silu, chain[0])
            e.reciprocal(silu[:, 2, :], silu[:, 1, :]).then_inc(s_silu, setup_step())
            e.wait_ge(s_silu, chain[0])
            e.tensor_tensor(silu[:, 1, :], silu[:, 0, :], silu[:, 2, :], ALU.mult).then_inc(s_silu, setup_step())
            e.wait_ge(s_silu, chain[0])
            e.tensor_copy(select[:, :, :], setup_select)
            e.tensor_copy(aug[POS_ROW:STACK, :, :], setup_aug[POS_ROW:STACK, :, :])
            e.tensor_copy(ident_bf[:, :], ident)
            e.tensor_copy(low_bf[:, :], square[:, 1, :])
            e.tensor_copy(upp_bf[:, :], square[:, 2, :])
            for n, which in enumerate((3, 2, 1, 2, 1, 2)):
                e.tensor_copy(mask_q2[:, n, :], square[:, which, :])
            for n in range(4):
                e.tensor_copy(mask_t2[:, n, :], square[:, 1 + n % 2, :])
            e.tensor_tensor(wqkv1[:, :, D:2 * D], wqkv1[:, :, D:2 * D],
                            x_res[:, 0:1, :].to_broadcast([P, KD, D]), ALU.mult).then_inc(s_silu, setup_step())
            e.wait_ge(s_silu, chain[0])
            half = HD2 // 2
            for l in range(DEPTH):
                e.tensor_scalar(x_ffn[:, l, 0:HD2], x_ffn[:, l, 0:HD2], QK_SCALE, None, ALU.mult).then_inc(s_silu, setup_step())
                e.wait_ge(s_silu, chain[0])
                for n in range(2):
                    scale = x_ffn[:, l, n * HD2:(n + 1) * HD2]
                    e.tensor_tensor(rot[:, l, 2 * n, :, :], rot[:, l, 2 * n, :, :],
                                    scale.rearrange("p (o d) -> p o d", o=1).to_broadcast([P, NT, HD2]), ALU.mult)
                    for a in range(2):
                        dst = rot[:, l, 2 * n + 1, :, a * half:(a + 1) * half]
                        s = scale[:, (1 - a) * half:(2 - a) * half]
                        e.tensor_tensor(dst, dst, s.rearrange("p (o d) -> p o d", o=1).to_broadcast([P, NT, half]), ALU.mult)
            e.wait_ge(s_silu_t, 1)
            e.tensor_copy(silu_t[:, :, :], bank[0][:, 0:KD * B].rearrange("p (k b) -> p k b", k=KD)).then_inc(s_silu_c, 1)
            e.wait_ge(s_mod, 1)
            for n in range(3):
                e.tensor_copy(mod_rows[:, 512 * n:512 * n + 512], bank[1 + n][0:B, :]).then_inc(s_silu, setup_step())
                e.wait_ge(s_silu, chain[0])
            for n in (1, 4):
                e.tensor_scalar(mod_rows[:, n * D:(n + 1) * D], mod_rows[:, n * D:(n + 1) * D], 1.0, None, ALU.add).then_inc(s_silu, setup_step())
                e.wait_ge(s_silu, chain[0])
            for n in (2, 5):
                row = mod_rows[:, n * D:(n + 1) * D]
                e.tensor_scalar(mod_abs[:, :], row, -1.0, None, ALU.mult).then_inc(s_silu, setup_step())
                e.wait_ge(s_silu, chain[0])
                e.tensor_tensor(mod_abs[:, :], mod_abs[:, :], row, ALU.max).then_inc(s_silu, setup_step())
                e.wait_ge(s_silu, chain[0])
                e.tensor_scalar(mod_abs[:, :], mod_abs[:, :], 0.25, None, ALU.max).then_inc(s_silu, setup_step())
                e.wait_ge(s_silu, chain[0])
                e.tensor_scalar(mod_sign[:, :], row, 0.0, 2.0, ALU.is_ge, ALU.mult).then_inc(s_silu, setup_step())
                e.wait_ge(s_silu, chain[0])
                e.tensor_scalar(mod_sign[:, :], mod_sign[:, :], -1.0, None, ALU.add).then_inc(s_silu, setup_step())
                e.wait_ge(s_silu, chain[0])
                e.tensor_tensor(row, mod_abs[:, :], mod_sign[:, :], ALU.mult).then_inc(s_silu, setup_step())
                e.wait_ge(s_silu, chain[0])
            e.tensor_copy(mod_abs[:, 0:1], mod_sign[:, 0:1]).then_inc(s_mod_r, 1)
            e.memset(wait_word[:, :], 0.0).then_inc(s_x3, 1)
            e.wait_ge(s_x3, 1)
            e.memset(wait_word[:, :], 0.0).then_inc(s_gx, 1)
            e.wait_ge(s_gx, 1)
            e.memset(wait_word[:, :], 0.0).then_inc(s_res, 1)
            e.wait_ge(s_res, 1)
            e.memset(wait_word[:, :], 0.0).then_inc(s_out, 16)
            e.wait_ge(s_out, 16)

            e.wait_ge(s_xn, 16)
            for t in range(NT):
                ins = e.bn_stats(stats[:, t, 0, :], y[:, t, :])
            ins.then_inc(s_silu, setup_step())
            e.wait_ge(s_silu, chain[0])
            for t in range(NT):
                ins = e.bn_aggr(mv[:, 1 + t, :], stats[:, t, 0, :])
            ins.then_inc(s_silu, setup_step())
            e.wait_ge(s_silu, chain[0])
            e.tensor_scalar(small[:, 0, :], mv[:, 1:1 + NT, 1], EPS, None, ALU.add).then_inc(s_var, 1)
            e.wait_ge(s_rstd, 1)
            for t in range(NT):
                e.tensor_scalar(y[:, t, :], y[:, t, :], mv[:, 1 + t, 0:1], rstd[:, t:t + 1],
                                ALU.subtract, ALU.mult).then_inc(s_yn, 1)

            with e.Fori(0, B) as i:
                tally = [0]

                def own_step():
                    tally[0] += 1
                    return 1

                def whole_stats(src, t0=0):
                    for t in range(NT):
                        e.bn_stats(stats[:, t, 0, :], src[:, t, :]).then_inc(s_vec, own_step())
                    e.wait_ge(s_vec, at(i, s_vec, tally[0]))
                    e.memset(wait_word[:, :], 0.0)
                    for t in range(NT):
                        e.bn_aggr(mv[:, 1 + t, :], stats[:, t, 0, :]).then_inc(s_vec, own_step())
                    e.wait_ge(s_vec, at(i, s_vec, tally[0]))
                    e.tensor_scalar(small[:, 0, :], mv[:, 1:1 + NT, 1], EPS, None, ALU.add).then_inc(s_var, 1)

                for j in range(4):
                    e.wait_ge(s_high, at(i, s_high, j + 1))
                    e.tensor_tensor(low1[:, j, :], bank[4 + j][:, :], high1[:, j, :].bitcast(F32),
                                    ALU.subtract).then_inc(s_low, 1)

                def maxima1(g, h):
                    for it in range(NT):
                        n = (g * G + h) * NT + it
                        e.wait_ge(s_s1, at(i, s_s1, n + 1))
                        e.tensor_reduce(neg_max[:, g % 2, h, it:it + 1], bank[(0, 1, 4)[n % 3]][:, it * P:T], AX_X, ALU.max,
                                        negate=True).then_inc(s_m1, 1)

                def heads1(g):
                    e.wait_ge(s_oq1, at(i, s_oq1, g + 1))
                    o = bank[7][:, :].rearrange("p (t h c) -> p t h c", t=NT, h=G)
                    rd = rden[:, 0, 0:NT * G].rearrange("p (t h o) -> p t h o", t=NT, o=1)
                    e.reciprocal(rd, o[:, :, :, HD1:HD1 + 1]).then_inc(s_vec, own_step())
                    e.wait_ge(s_vec, at(i, s_vec, tally[0]))
                    e.tensor_tensor(on1[:, :, g * G * HD1:(g + 1) * G * HD1].rearrange("p t (h c) -> p t h c", h=G),
                                    o[:, :, :, 0:HD1], rd.to_broadcast([P, NT, G, HD1]), ALU.mult).then_inc(s_on1, 1)

                def copy1(g):
                    e.wait_ge(s_pv1, at(i, s_pv1, (g + 1) * NT))
                    e.tensor_copy(oT1[:, g % 2, :], bank[5 + g % 2][:, :]).then_inc(s_o1, 1)

                for h in range(G):
                    maxima1(0, h)
                for g in range(NG1):
                    for step in range(NT):
                        if step == 1 and g >= 1:
                            copy1(g - 1)
                        if step == 2 and g >= 1:
                            heads1(g - 1)
                        if g + 1 < NG1:
                            maxima1(g + 1, step)
                copy1(NG1 - 1)
                heads1(NG1 - 1)
                e.wait_ge(s_x, at(i, s_x, 16))
                for n in range(2):
                    e.wait_ge(s_p1, at(i, s_p1, n + 1))
                    e.tensor_tensor(x_res[:, 2 * n:2 * n + 2, :], bank[2 + n][:, :].rearrange("p (t f) -> p t f", t=2),
                                    x_res[:, 2 * n:2 * n + 2, :], ALU.add).then_inc(s_x1, 1)
                e.wait_ge(s_x1, at(i, s_x1, 2))
                whole_stats(x_res)
                for t in range(NT):
                    e.scalar_tensor_tensor(x_ffn[:, t, :], x_res[:, t, :], mv[:, 1 + t, 0:1], mod_row[:, 2, :],
                                           ALU.subtract, ALU.mult).then_inc(s_vec, own_step())
                e.wait_ge(s_vec, at(i, s_vec, tally[0]))
                e.wait_ge(s_rstd, at(i, s_rstd, 1))
                for t in range(NT):
                    e.scalar_tensor_tensor(x_ffn[:, t, :], x_ffn[:, t, :], rstd[:, t:t + 1], mod_row[:, 1, :],
                                           ALU.mult, ALU.add).then_inc(s_xf, 1)

                for l in range(DEPTH):
                    e.wait_ge(s_xT, at(i, s_xT, l + 1))
                    e.tensor_copy(hT[:, 1, 1:T], bank[1][:, 0:T - 1]).then_inc(s_sTd, 1)

                    sum_done = {}

                    def scaled(t):
                        for n in range(2):
                            e.wait_ge(s_rn, at(i, s_rn, (l * NT + t) * 2 + n + 1))
                            e.wait_ge(s_rsum, at(i, s_rsum, pool_sums(l, t, n)))
                            if not on_pool(t, n):
                                e.wait_ge(s_vec, at(i, s_vec, sum_done[t]))
                            dst = (q2, k2)[n][:, t, :].rearrange("p (h d) -> p h d", h=H2)
                            r = rnorm[:, t % 2, n * H2:(n + 1) * H2].rearrange("p (h o) -> p h o", o=1)
                            e.tensor_tensor(dst, dst, r.to_broadcast([P, H2, HD2]), ALU.mult).then_inc(s_qn, 1)

                    for t in range(NT):
                        for n in range(2):
                            k = (l * NT + t) * 2 + n
                            e.wait_ge(s_qk2, at(i, s_qk2, k + 1))
                            if t >= 1:
                                e.wait_ge(s_rsum, at(i, s_rsum, pool_sums(l, t - 1, n)))
                                if not on_pool(t - 1, n):
                                    e.wait_ge(s_vec, at(i, s_vec, sum_done[t - 1]))
                            src = bank[2 + n + 3 * (t % 2)][:, :].rearrange("p (h a d) -> p h a d", h=H2, a=2)
                            cos = rot[:, l, 2 * n, t, :].rearrange("p (o a d) -> p o a d", o=1, a=2)
                            sin = rot[:, l, 2 * n + 1, t, :].rearrange("p (o a d) -> p o a d", o=1, a=2)
                            to = "p (h a d) -> p h a d"
                            e.wait_ge(s_sq, at(i, s_sq, k + 1))
                            e.tensor_tensor(rot_c[:, n, :].rearrange(to, h=H2, a=2), src,
                                            cos.to_broadcast([P, H2, 2, HD2 // 2]), ALU.mult)
                            e.tensor_tensor(rot_s[:, n, :].rearrange(to, h=H2, a=2), src[:, :, ::-1, :],
                                            sin.to_broadcast([P, H2, 2, HD2 // 2]), ALU.mult).then_inc(s_rt, 1)
                            e.tensor_reduce(ssq[:, t % 2, n * H2:(n + 1) * H2],
                                            sq[:, n, :].rearrange("p (h d) -> p h d", h=H2), AX_X, ALU.add).then_inc(s_vec, own_step())
                            e.wait_ge(s_vec, at(i, s_vec, tally[0]))
                            heads = slice(n * H2, (n + 1) * H2)
                            e.tensor_scalar(ssq[:, t % 2, heads], ssq[:, t % 2, heads], 1e-24, None,
                                            ALU.max).then_inc(s_ss, 1)
                        if not on_pool(t, 1):
                            e.tensor_tensor(k2[:, t, :], rot_c[:, 1, :], rot_s[:, 1, :], ALU.add).then_inc(s_vec, own_step())
                            sum_done[t] = tally[0]
                        if t >= 1:
                            scaled(t - 1)
                    scaled(NT - 1)

                    def low2(pair):
                        for n in range(2):
                            for a in range(2):
                                h = 2 * pair + a
                                own, other = slice(64 * a, 64 * a + 64), slice(64 - 64 * a, 128 - 64 * a)
                                e.wait_ge(s_hi2, at(i, s_hi2, (l * H2 // 2 + pair) * 6 + (1 + a if n == 0 else 4 + 2 * a)))
                                high = (q2_stack, k2_high)[n]
                                dst = q2_stack[other, h, :] if n == 0 else k2_low[own, h, :]
                                e.tensor_tensor(dst, bank[n][own, :], high[own, h, :].bitcast(F32),
                                                ALU.subtract).then_inc(s_lo2, 1)

                    def maxima2(h):
                        for n in range(2):
                            k = (l * H2 + h) * 2 + n
                            e.wait_ge(s_s2, at(i, s_s2, k + 1))
                            e.tensor_reduce(neg_max2[:, h % 2, 2 * n:2 * n + 2],
                                            bank[2 + n][:, :].rearrange("p (t k) -> p t k", t=2), AX_X, ALU.max,
                                            negate=True).then_inc(s_m2, 1)

                    def copy2(pair):
                        k = l * H2 // 2 + pair
                        e.wait_ge(s_pv2, at(i, s_pv2, k + 1))
                        e.tensor_copy(oT2[:, pair, :], bank[6][:, :]).then_inc(s_o2, 1)
                        if pair % 2:
                            e.tensor_copy(denT2[:, pair // 2, :], bank[7][:, :]).then_inc(s_dn, 1)

                    low2(0)
                    for h in range(H2):
                        maxima2(h)
                        if h % 2 == 0 and h // 2 + 1 < H2 // 2:
                            low2(h // 2 + 1)
                        if h >= 3 and h % 2:
                            copy2(h // 2 - 1)
                    copy2(H2 // 2 - 1)
                    for n in range(2):
                        e.wait_ge(s_dT, at(i, s_dT, l * 2 + n + 1))
                        e.reciprocal(rden[:, n, :].rearrange("p (k o) -> p k o", o=1),
                                     bank[n][:, :].rearrange("p (k c) -> p k c", c=32)[:, :, 0:1]).then_inc(s_vec, own_step())
                    e.wait_ge(s_vec, at(i, s_vec, tally[0]))
                    for it in range(NT):
                        e.wait_ge(s_oq2, at(i, s_oq2, l * NT + it + 1))
                        r = rden[:, it // 2, (it % 2) * H2:(it % 2 + 1) * H2].rearrange("p (h o) -> p h o", o=1)
                        e.tensor_tensor(on2[:, it, :].rearrange("p (h d) -> p h d", h=H2),
                                        bank[2 + it][:, :].rearrange("p (h d) -> p h d", h=H2),
                                        r.to_broadcast([P, H2, HD2]), ALU.mult).then_inc(s_on2, 1)
                    for k in (1, 3):
                        e.wait_ge(s_onT2, at(i, s_onT2, l * 4 + k + 1))
                        e.tensor_copy(onT2[:, k, :], bank[(6, 7, 0, 1)[k]][:, :]).then_inc(s_onTd2, 1)
                    for n in range(2):
                        e.wait_ge(s_p2, at(i, s_p2, l * 2 + n + 1))
                        e.tensor_tensor(x_ffn[:, 2 * n:2 * n + 2, :], bank[2 + n][:, :].rearrange("p (t f) -> p t f", t=2),
                                        x_ffn[:, 2 * n:2 * n + 2, :], ALU.add).then_inc(s_x2, 1)
                        e.wait_ge(s_x2, at(i, s_x2, l * 2 + n + 1))
                        for t in (2 * n, 2 * n + 1):
                            for a in range(2):
                                e.bn_stats(stats[:, t, a, :], x_ffn[:, t, a * P:(a + 1) * P]).then_inc(s_vec, own_step())
                    e.wait_ge(s_vec, at(i, s_vec, tally[0]))
                    e.memset(wait_word[:, :], 0.0)
                    for t in range(NT):
                        e.bn_aggr(mv1[:, t, :], stats[:, t, 0, :]).then_inc(s_vec, own_step())
                    for t in range(NT):
                        ins = e.bn_aggr(mv[:, 1 + t, :], stats[:, t, 1, :])
                    ins.then_inc(s_st, 1)
                    e.wait_ge(s_dshift, at(i, s_dshift, l + 1))
                    moved = bank[0][:, 0:2 * NT].rearrange("p (t c) -> p t c", c=2)
                    mean2, var2, delta, mean, quarter, var = (small[:, n, :] for n in (0, 1, 2, 3, 4, 5))
                    e.tensor_tensor(delta, moved[:, :, 0], mv1[:, :, 0], ALU.subtract).then_inc(s_vec, own_step())
                    e.tensor_tensor(mean2, moved[:, :, 0], mv1[:, :, 0], ALU.add).then_inc(s_vec, own_step())
                    e.tensor_tensor(var2, moved[:, :, 1], mv1[:, :, 1], ALU.add).then_inc(s_vec, own_step())
                    e.wait_ge(s_vec, at(i, s_vec, tally[0]))
                    e.tensor_scalar(mean, mean2, 0.5, None, ALU.mult).then_inc(s_vec, own_step())
                    e.tensor_scalar(var2, var2, 0.5, EPS, ALU.mult, ALU.add).then_inc(s_vec, own_step())
                    e.scalar_tensor_tensor(quarter, delta, 0.25, delta, ALU.mult, ALU.mult).then_inc(s_vec, own_step())
                    e.wait_ge(s_vec, at(i, s_vec, tally[0]))
                    e.tensor_tensor(var, quarter, var2, ALU.add).then_inc(s_var, 1)
                    e.wait_ge(s_rstd, at(i, s_rstd, 2 + l))
                    e.tensor_copy(shift_up[:, 0, 0:NT], rstd[:, :]).then_inc(s_vec, own_step())
                    e.tensor_tensor(shift_up[:, 1, 0:NT], rstd[:, :], mean, ALU.mult).then_inc(s_vec, own_step())
                    e.wait_ge(s_vec, at(i, s_vec, tally[0]))
                    e.tensor_copy(shift_up[:, 1, NT:NT + 1], shift_up[:, 1, 0:1]).then_inc(s_up, 1)
                    for t in range(NT):
                        e.tensor_scalar(y[:, t, 0:P], x_ffn[:, t, 0:P], mean[:, t:t + 1], rstd[:, t:t + 1],
                                        ALU.subtract, ALU.mult).then_inc(s_vec, own_step())
                    e.wait_ge(s_ushift, at(i, s_ushift, l + 1))
                    e.tensor_copy(small[:, 6:8, :], bank[1][:, 0:2 * NT].rearrange("p (c t) -> p c t", c=2)).then_inc(s_vec, own_step())
                    e.wait_ge(s_vec, at(i, s_vec, tally[0]))
                    for t in range(NT):
                        e.tensor_scalar(y[:, t, P:2 * P], x_ffn[:, t, P:2 * P], small[:, 6, t:t + 1], small[:, 7, t:t + 1],
                                        ALU.mult, ALU.subtract).then_inc(s_y, 1)
                    e.wait_ge(s_nT, at(i, s_nT, l + 1))
                    e.tensor_scalar(hT[:, 1, 1:T], bank[1][:, 0:T - 1], lng[:, l, 1:2], lnb[:, l, 1:2],
                                    ALU.mult, ALU.add).then_inc(s_nTd, 1)
                    e.tensor_scalar(hT[:, 1, 0:1], bank[1][:, T - 1:T], lng[:, l, 1:2], lnb[:, l, 1:2],
                                    ALU.mult, ALU.add).then_inc(s_nTd, 1)
                    for m in range(HT):
                        r = P if m < HT - 1 else HREST
                        e.wait_ge(s_a, at(i, s_a, l * HT + m + 1))
                        e.wait_ge(s_gl, at(i, s_gl, l * HT + m + 1))
                        e.scalar_tensor_tensor(u[0:r, m, :], bank[3 + 2 * (m % 2)][0:r, :], b1[0:r, l, 0, m:m + 1],
                                               gate[0:r, m % 2, :], ALU.add, ALU.mult).then_inc(s_u, 1)
                        if l == DEPTH - 1 and m == HT - 3:
                            e.wait_ge(s_xn, at(i, s_xn, 16))
                            whole_stats(y)
                        if l == DEPTH - 1 and m == HT - 1:
                            e.wait_ge(s_rstd, at(i, s_rstd, 4))
                            for t in range(NT):
                                e.tensor_scalar(y[:, t, :], y[:, t, :], mv[:, 1 + t, 0:1], rstd[:, t:t + 1],
                                                ALU.subtract, ALU.mult).then_inc(s_yn, 1)
                    for n in range(2):
                        e.wait_ge(s_f, at(i, s_f, l * 2 + n + 1))
                        e.wait_ge(s_bias, at(i, s_bias, l * 2 + 2))
                        e.tensor_tensor(x_ffn[:, 2 * n:2 * n + 2, :], bank[6 + n][:, :].rearrange("p (t f) -> p t f", t=2),
                                        x_ffn[:, 2 * n:2 * n + 2, :], ALU.add).then_inc(s_x3, 1)
                e.wait_ge(s_gx, at(i, s_gx, 1))
                e.tensor_tensor(x_res[:, :, :], x_ffn[:, :, :], x_res[:, :, :], ALU.add).then_inc(s_res, 1)
                assert tally[0] == VEC, tally[0]

        @block.tensor
        def _(e):
            e.wait_ge(s_const, N_CONST[0])
            e.wait_ge(s_silu, 3)
            for k in range(KD):
                ins = e.transpose(bank[0][:, k * B:(k + 1) * B], silu[:, 1, k * P:(k + 1) * P], ident[0:B, 0:B])
            ins.then_inc(s_silu_t, 1)
            e.wait_ge(s_silu_c, 1)
            for n in range(3):
                for k in range(KD):
                    ins = e.matmul(bank[1 + n][0:B, :], silu_t[:, k, :], wmod[:, k, 512 * n:512 * n + 512],
                                   start=(k == 0), stop=(k == KD - 1))
            ins.then_inc(s_mod, 1)
            e.wait_ge(s_cst_dve, 2)
            e.wait_ge(s_mod_r, 1)

            with e.Fori(0, B) as i:
                for t in range(NT):
                    e.wait_ge(s_yn, at(i, s_yn, t + 1 - NT))
                    for k in range(KD):
                        ins = e.transpose(bank[k][:, t * P:(t + 1) * P], y[:, t, k * P:(k + 1) * P], ident)
                ins.then_inc(s_yT, 1)

                def project1(j):
                    col = (j % 2) * D + (j // 2) * P
                    for k in range(KD):
                        ins = e.matmul(bank[4 + j][:, :], wqkv1[:, k, col:col + P], hT[:, k, :],
                                       start=(k == 0), stop=(k == KD - 1))
                    ins.then_inc(s_qk, 1)

                def stack_rows(g, which):
                    m = g * G + which
                    rows = slice(64 * (g % 2) + 32 * (which // 2), 64 * (g % 2) + 32 * (which // 2) + 32)
                    j, n = 2 * (g // 2) + which % 2, which % 2
                    e.wait_ge(s_low, at(i, s_low, 4 if g == 1 else 2 * (g // 2) + 2))
                    if m == 2 or m == 3:
                        e.wait_ge(s_stk, at(i, s_stk, m - 1))
                    elif g:
                        e.wait_ge(s_stk, at(i, s_stk, m))
                        if g == RING and which >= 2:
                            e.wait_ge(s_on1, at(i, s_on1, 1))
                    b = bank[m % 2 if g == 0 else 7]
                    e.matmul(b[:, :], select[rows, 2 * n, :], high1[rows, j, :], start=True, stop=False)
                    e.matmul(b[:, :], select[rows, 2 * n + 1, :], low1[rows, j, :], start=False,
                             stop=True).then_inc(s_sel, 1)

                def scores1(g, h, it):
                    q, k = q_ring[g % RING], k_ring[g % RING]
                    n = (g * G + h) * NT + it
                    if g == 0 and h == 0 and it == 0:
                        e.wait_ge(s_stk, at(i, s_stk, G))
                        e.wait_ge(s_aug, at(i, s_aug, 16 * 2 * RING))
                    elif it == 0:
                        e.wait_ge(s_stk, at(i, s_stk, g * G + h // 2 * 2 + 2))
                    if n >= 3:
                        e.wait_ge(s_m1, at(i, s_m1, n - 2))
                    b = bank[(0, 1, 4)[n % 3]]
                    e.matmul(b[:, it * P:T], q[0:STACK, h, it * P:(it + 1) * P],
                             k[0:STACK, h, it * P:T], start=True, stop=False, skip_group_check=True)
                    e.matmul(b[:, it * P:(it + 1) * P], ident_bf[:, :], low_bf[:, :], start=False, stop=True,
                             skip_group_check=True).then_inc(s_s1, 1)

                def key_scores1(g, kt, h):
                    q, k, slot = q_ring[g % RING], k_ring[g % RING], (g * G + h) % 8
                    n = (g * NT + NT - 1 - kt) * G + h
                    if n >= 2:
                        e.wait_ge(s_e1, at(i, s_e1, n - 1))
                    elif n == 0:
                        e.wait_ge(s_v1, at(i, s_v1, 2))
                        e.wait_ge(s_low, at(i, s_low, 4))
                    e.wait_ge(s_d1, at(i, s_d1, g * G + h + 1))
                    b, w = bank[2 + n % 2], (kt + 1) * P
                    e.matmul(b[:, 0:w], k[0:STACK, h, kt * P:w], q[0:STACK, h, 0:w],
                             start=True, stop=False, skip_group_check=True)
                    e.matmul(b[:, 0:w], ones_bf[:, :], diag1[slot][:, 0:w], start=False, stop=False,
                             skip_group_check=True)
                    e.matmul(b[:, kt * P:w], ident_bf[:, :], upp_bf[:, :], start=False, stop=True,
                             skip_group_check=True).then_inc(s_t1, 1)

                def values1(g, kt):
                    w = (kt + 1) * P
                    e.wait_ge(s_e1, at(i, s_e1, (g * NT + NT - kt) * G))
                    if kt == NT - 1 and g >= 2:
                        e.wait_ge(s_o1, at(i, s_o1, g - 1))
                    if kt == NT - 1 and g == 0:
                        e.wait_ge(s_v1one, at(i, s_v1one, 1))
                    for h in range(G):
                        ins = e.matmul(bank[5 + g % 2][32 * h:32 * h + 32, 0:w], v1[:, kt, g * G + h, :],
                                       probs1[:, kt % 2, h, 0:w], start=(kt == NT - 1), stop=(kt == 0),
                                       skip_group_check=True)
                    ins.then_inc(s_pv1, 1)

                def back1(g):
                    e.wait_ge(s_o1, at(i, s_o1, g + 1))
                    e.wait_ge(s_stk, at(i, s_stk, min(G * NG1, (g + 3) * G + 2)))
                    if g >= 1:
                        e.wait_ge(s_on1, at(i, s_on1, g))
                    for it in range(NT):
                        ins = e.transpose(bank[7][:, it * P:(it + 1) * P], oT1[:, g % 2, it * P:(it + 1) * P], ident)
                    ins.then_inc(s_oq1, 1)

                e.wait_ge(s_hT, at(i, s_hT, KD))
                project1(0)
                project1(1)
                for t in range(NT):
                    for k in range(KD):
                        ins = e.matmul(bank[2 + t // 2][:, (t % 2) * D:(t % 2 + 1) * D], hT[:, k, t * P:(t + 1) * P],
                                       wqkv1[:, k, 2 * D:3 * D], start=(k == 0), stop=(k == KD - 1))
                    if t % 2:
                        ins.then_inc(s_v, 1)
                e.wait_ge(s_x3, at(i, s_x3, 0))
                for j in (2, 3):
                    stack_rows(0, 2 * j - 4)
                    stack_rows(0, 2 * j - 3)
                    project1(j)
                for h in range(G):
                    for it in range(NT):
                        scores1(0, h, it)
                        if it == 1:
                            stack_rows(1, h)
                for g in range(NG1):
                    unit = 0
                    for step in range(NT):
                        kt = NT - 1 - step
                        for h in range(G):
                            key_scores1(g, kt, h)
                            for _ in range(SPREAD[step][h] if g + 1 < NG1 else 0):
                                scores1(g + 1, unit // NT, unit % NT)
                                unit += 1
                            if h == 1 and g + 2 < NG1:
                                stack_rows(g + 2, step)
                            if h == 1 and step == 1 and g:
                                back1(g - 1)
                        if step:
                            values1(g, kt + 1)
                        elif g:
                            values1(g - 1, 0)
                values1(NG1 - 1, 0)
                back1(NG1 - 1)
                e.wait_ge(s_on1, at(i, s_on1, NG1))
                for t in range(NT):
                    for k in range(KD):
                        ins = e.transpose(bank[k][:, t * P:(t + 1) * P], on1[:, t, k * P:(k + 1) * P], ident)
                ins.then_inc(s_onT1, 1)
                e.wait_ge(s_onTc1, at(i, s_onTc1, KD))
                e.wait_ge(s_wg, at(i, s_wg, 1))
                for t in range(NT):
                    for k in range(KD):
                        ins = e.matmul(bank[2 + t // 2][:, (t % 2) * D:(t % 2 + 1) * D], onT1[:, k, t * P:(t + 1) * P],
                                       wout_g[:, k, :], start=(k == 0), stop=(k == KD - 1))
                    if t % 2:
                        ins.then_inc(s_p1, 1)

                for l in range(DEPTH):
                    for t in range(NT):
                        if l == 0:
                            e.wait_ge(s_xf, at(i, s_xf, t + 1))
                        elif t % 2 == 0:
                            e.wait_ge(s_x3, at(i, s_x3, 2 * l - 1 + t // 2))
                        for k in range(KD):
                            ins = e.transpose(bank[k][:, t * P:(t + 1) * P], x_ffn[:, t, k * P:(k + 1) * P], ident)
                    ins.then_inc(s_xT, 1)
                    e.wait_ge(s_sT, at(i, s_sT, l + 1))
                    e.wait_ge(s_sTd, at(i, s_sTd, l + 1))
                    e.wait_ge(s_zero, at(i, s_zero, l + 1))
                    e.wait_ge(s_lw[0], at(i, s_lw[0], 16 * (l + 1)))
                    for t, what in PROJECTIONS:
                        for n in ((0, 1) if what == "qk" else (2,)):
                            b = bank[2 + n + 3 * (t % 2)]
                            if t >= 2:
                                if n < 2:
                                    e.wait_ge(s_rt, at(i, s_rt, (l * NT + t - 2) * 2 + n + 1))
                                else:
                                    e.wait_ge(s_v2, at(i, s_v2, l * NT + t - 1))
                            for k in range(KD):
                                ins = e.matmul(b[:, :], hT[:, k, t * P:(t + 1) * P],
                                               wqkv2[:, k, n * INNER:(n + 1) * INNER], start=(k == 0), stop=(k == KD - 1))
                            ins.then_inc(s_qk2 if n < 2 else s_vp2, 1)

                    def turn_pair(pair):
                        for n, src in enumerate((q2, k2)):
                            if pair == 0:
                                e.wait_ge(s_qn, at(i, s_qn, (l + 1) * NT * 2))
                            else:
                                e.wait_ge(s_lo2, at(i, s_lo2, (l * H2 // 2 + pair - 1) * 4 + 2 * n + 2))
                            for t in range(NT):
                                ins = e.transpose(bank[n][:, t * P:(t + 1) * P], src[:, t, pair * P:(pair + 1) * P], ident)
                            ins.then_inc(s_tq, 1)

                    def scores2(h):
                        for n in range(2):
                            k = (l * H2 + h) * 2 + n
                            b = bank[2 + n]
                            e.wait_ge(s_lo2, at(i, s_lo2, (l * H2 // 2 + h // 2 + 1) * 4))
                            if h:
                                e.wait_ge(s_m2, at(i, s_m2, k - 1))
                            e.matmul(b[:, :], ident_bf[:, :], mask_q2[:, 2 * n:2 * n + 4, :], start=True, stop=False,
                                     skip_group_check=True)
                            for it in (2 * n, 2 * n + 1):
                                a = max(it - 1, 0) * P
                                to = (it % 2) * 2 * P + (P if it == 0 else 0)
                                ins = e.matmul(b[:, to:(it % 2 + 1) * 2 * P], q2_stack[:, h, it * P:(it + 1) * P],
                                               k2_high[:, h, a:(it + 1) * P], start=False, stop=(it % 2 == 1),
                                               skip_group_check=True)
                            ins.then_inc(s_s2, 1)

                    def key_scores2(h):
                        e.wait_ge(s_d2, at(i, s_d2, l * H2 + h + 1))
                        if h == 0:
                            e.wait_ge(s_klow0, at(i, s_klow0, 2))
                        for n in range(2):
                            k = (l * H2 + h) * 2 + n
                            w = (512, 384)[n]
                            b = bank[4 + n]
                            if h:
                                e.wait_ge(s_e2, at(i, s_e2, k - 1))
                            e.matmul(b[:, 0:w], ident_bf[:, :], mask_t2[:, 0:w // P, :], start=True, stop=False,
                                     skip_group_check=True)
                            for kt in (2 * n, 2 * n + 1):
                                c = (kt % 2) * 2 * P
                                q = slice(kt * P, min(kt + 2, NT) * P)
                                to = b[:, c:c + q.stop - q.start]
                                for left in (k2_high, k2_low):
                                    e.matmul(to, left[:, h, kt * P:(kt + 1) * P], q2_stack[:, h, q], start=False, stop=False,
                                             skip_group_check=True)
                                ins = e.matmul(to, ones_bf[:, :], diag[:, h % G, q], start=False, stop=(kt % 2 == 1),
                                               skip_group_check=True)
                            ins.then_inc(s_t2, 1)

                    def values2(pair):
                        k = l * H2 // 2 + pair
                        e.wait_ge(s_e2, at(i, s_e2, (l * H2 + 2 * pair + 2) * 2))
                        if pair:
                            e.wait_ge(s_o2, at(i, s_o2, k))
                        if pair == 0:
                            e.wait_ge(s_v2, at(i, s_v2, (l + 1) * NT))
                        if pair == 2:
                            e.wait_ge(s_dn, at(i, s_dn, l * 2 + 1))
                        for kt in range(NT):
                            q = slice(kt * P, min(kt + 2, NT) * P)
                            w = q.stop - q.start
                            for h in (2 * pair, 2 * pair + 1):
                                e.matmul(bank[6][64 * (h % 2):64 * (h % 2) + 64, q], v2[:, kt, h * HD2:(h + 1) * HD2],
                                         probs2[h % 4][:, kt * 256:kt * 256 + w], start=(kt == 0), stop=(kt == NT - 1),
                                         skip_group_check=True)
                            for h in (2 * pair, 2 * pair + 1):
                                c = 32 * (h % 4)
                                ins = e.matmul(bank[7][c:c + 32, q], ones32[:, :],
                                               probs2[h % 4][:, kt * 256:kt * 256 + w], start=(kt == 0), stop=(kt == NT - 1),
                                               skip_group_check=True)
                        ins.then_inc(s_pv2, 1)

                    turn_pair(0)
                    for h in range(H2):
                        scores2(h)
                        if h % 2 == 0 and h // 2 + 1 < H2 // 2:
                            turn_pair(h // 2 + 1)
                        if h >= 1:
                            key_scores2(h - 1)
                        if h >= 3 and h % 2:
                            values2((h - 3) // 2)
                    key_scores2(H2 - 1)
                    values2(H2 // 2 - 1)
                    e.wait_ge(s_dn, at(i, s_dn, l * 2 + 2))
                    for it in range(NT):
                        for a in range(2):
                            c = ((it % 2) * 2 + a) * P
                            ins = e.transpose(bank[it // 2][:, c:c + P], denT2[:, a, it * P:(it + 1) * P], ident)
                        if it % 2:
                            ins.then_inc(s_dT, 1)
                    for it in range(NT):
                        for k in range(H2 // 2):
                            ins = e.transpose(bank[2 + it][:, k * P:(k + 1) * P], oT2[:, k, it * P:(it + 1) * P], ident)
                        ins.then_inc(s_oq2, 1)
                    for it in range(NT):
                        e.wait_ge(s_on2, at(i, s_on2, l * NT + it + 1))
                        for k in range(4):
                            ins = e.transpose(bank[(6, 7, 0, 1)[k]][:, it * P:(it + 1) * P],
                                              on2[:, it, k * P:(k + 1) * P], ident)
                            if it == NT - 1:
                                ins.then_inc(s_onT2, 1)
                    e.wait_ge(s_onTc2, at(i, s_onTc2, (l + 1) * 2))
                    e.wait_ge(s_onTd2, at(i, s_onTd2, (l + 1) * 2))
                    e.wait_ge(s_lw[1], at(i, s_lw[1], 16 * (l + 1)))
                    for t in range(NT):
                        for k in range(4):
                            ins = e.matmul(bank[2 + t // 2][:, (t % 2) * D:(t % 2 + 1) * D], onT2[:, k, t * P:(t + 1) * P],
                                           wo[:, k, :], start=(k == 0), stop=(k == 3))
                        if t % 2:
                            ins.then_inc(s_p2, 1)
                    e.wait_ge(s_st, at(i, s_st, l + 1))
                    moved = bank[0][:, 0:2 * NT]
                    e.matmul(moved, down, mv[:, 1:1 + NT, :], start=True, stop=False)
                    e.matmul(moved, down_wrap, mv[:, 0:NT, :], start=False, stop=True).then_inc(s_dshift, 1)
                    e.wait_ge(s_up, at(i, s_up, l + 1))
                    moved = bank[1][:, 0:2 * NT]
                    e.matmul(moved, up, shift_up[:, :, 0:NT], start=True, stop=False)
                    e.matmul(moved, up_wrap, shift_up[:, :, 1:1 + NT], start=False, stop=True).then_inc(s_ushift, 1)
                    for t in range(NT):
                        e.wait_ge(s_y, at(i, s_y, NT * l + t + 1))
                        for k in range(KD):
                            ins = e.transpose(bank[k][:, t * P:(t + 1) * P], y[:, t, k * P:(k + 1) * P], ident)
                    ins.then_inc(s_nT, 1)
                    e.wait_ge(s_nTc, at(i, s_nTc, l + 1))
                    e.wait_ge(s_nTd, at(i, s_nTd, 2 * (l + 1)))
                    e.wait_ge(s_lw[2], at(i, s_lw[2], 16 * (l + 1)))
                    for m in range(HT):
                        r = P if m < HT - 1 else HREST
                        for half, done in ((1, s_g), (0, s_a)):
                            b = bank[(3, 2)[half] + 2 * (m % 2)]
                            if m >= 2:
                                e.wait_ge(s_u, at(i, s_u, l * HT + m - 1))
                            for k in range(KD):
                                ins = e.matmul(b[0:r, :], w1[:, k, half * HID + m * P:half * HID + m * P + r], hT[:, k, :],
                                               start=(k == 0), stop=(k == KD - 1))
                            ins.then_inc(done, 1)
                    e.wait_ge(s_u, at(i, s_u, (l + 1) * HT))
                    e.wait_ge(s_lw[3], at(i, s_lw[3], 32 * (l + 1)))
                    for t in range(NT):
                        for m in range(HT):
                            r = P if m < HT - 1 else HREST
                            ins = e.matmul(bank[6 + t // 2][:, (t % 2) * D:(t % 2 + 1) * D],
                                           u[0:r, m, t * P:(t + 1) * P], w2[0:r, m, :],
                                           start=(m == 0), stop=(m == HT - 1))
                        if t % 2:
                            ins.then_inc(s_f, 1)


_INS = ['L0_attn_x', 'L0_attn_W_qkv', 'L0_attn_W_out', 'L0_ffn_wqkv', 'L0_ffn_q_scale', 'L0_ffn_k_scale',
        'L0_ffn_wo', 'L0_ffn_ln_g', 'L0_ffn_ln_b', 'L0_ffn_w1', 'L0_ffn_b1', 'L0_ffn_w2', 'L0_ffn_b2', 'L0_c',
        'L0_wmod']


def _constants(tokens, dim):
    import numpy as np

    n = np.arange(P)
    row, col = n[:, None], n[None, :]
    square = np.stack([
        row == col,
        np.where(col < row, NEG, 0.0),
        np.where(col > row, NEG, 0.0),
        np.full((P, P), NEG),
        col == row + 1,
        (row == P - 1) & (col == 0),
        col == row - 1,
        (row == 0) & (col == P - 1),
    ], axis=1).astype(np.float32)
    tiles = tokens // P
    t = np.arange(tokens)
    aug = np.zeros((32, 2, tokens), np.float32)
    aug[0, 0], aug[0, 1] = t % P, 1
    aug[1, 0], aug[1, 1] = 1, -(t % P)
    for a in range(tiles):
        aug[2 + a, 0] = t // P == a
        aug[2 + a, 1] = -P * (t // P - a)
    select = np.zeros((P, 4, 2, 4, 16), np.float32)
    for a in range(P // 32):
        for pair in range(2):
            for r in range(16):
                for which, blocks in enumerate(((0, 2), (1, 3), (0, 1), (2, 3))):
                    select[32 * a + 16 * pair + r, which, pair, blocks, r] = 1
    select = select.reshape(P, 4, P)
    heads = 16
    kscale = np.repeat(0.25 / np.array(slopes(heads)), dim // heads)[None, :].astype(np.float32)
    d, window = 64, 128
    f = np.float32
    half = np.arange(0, d, 2, dtype=f)
    inv = f(1.0) / np.power(f(10000.0), half / f(d))
    tt = np.arange(tokens, dtype=f)
    freq = tt[:, None] * inv[None, :]
    freq = np.concatenate([freq, freq], -1)
    base = (half + f(0.4 * d)) / f(1.4 * d)
    power = (tt - f(tokens // 2)) / f(window // 2)
    scale = np.power(base[None, :], power[:, None])
    scale = np.concatenate([scale, scale], -1)
    sign = np.where(np.arange(d) < d // 2, f(-1), f(1))
    cos, sin = np.cos(freq), np.sin(freq) * sign
    rot = np.stack([cos * scale, sin * scale, cos / scale, sin / scale]).astype(np.float32)
    rot = rot.reshape(4, tiles, P, d).transpose(2, 0, 1, 3)
    return {"square": square, "aug": aug, "select": select, "rot": np.ascontiguousarray(rot), "kscale": kscale}


def kernel(**inputs):
    import numpy as _np
    import concourse.bacc as _bacc
    from concourse import mybir as _mybir
    from concourse.bass_utils import run_bass_kernel_spmd as _run

    nc = _bacc.Bacc("TRN2", target_bir_lowering=False, num_devices=1)
    arrays, args = {}, []
    batch, tokens, dim = inputs['L0_attn_x'].shape
    data = [(n, inputs[n]) for n in _INS] + list(_constants(tokens, dim).items())
    for name, value in data:
        a = _np.ascontiguousarray(value)
        arrays[f"in_{name}_dram"] = a
        args.append(nc.dram_tensor(f"in_{name}_dram", a.shape, _mybir.dt.from_np(a.dtype), kind="ExternalInput").ap())
    out = nc.dram_tensor("out_0_dram", (batch, tokens, dim), _mybir.dt.float32, kind="ExternalOutput").ap()
    adaln_block(nc, *args, out)
    r = _run(nc, [arrays], core_ids=[0])
    return r.results[0]["out_0_dram"]
```
